# Optimizing a Trainium2 kernel written in Bass

```python
import numpy as np
import jax
import jax.numpy as jnp

def _softmax(x, axis=-1):
    return jax.nn.softmax(x, axis=axis)

def _gelu(x):
    return jax.nn.gelu(x, approximate=True)

def _silu(x):
    return jax.nn.silu(x)

def _sigmoid(x):
    return jax.nn.sigmoid(x)

def _layernorm(x, axis=-1, eps=1e-05):
    m = jnp.mean(x, axis=axis, keepdims=True)
    v = jnp.var(x, axis=axis, keepdims=True)
    return (x - m) / jnp.sqrt(v + eps)

def _scatter_add(tgt, idx, src, axis=0):
    return tgt.at[idx].add(src)

def _segment_sum(src, seg, n):
    return jax.ops.segment_sum(src, seg, n)
kernel_name = 'mk_adaln_ffn_d1_seqx_r8_f8005f'

def setup_inputs(seed: int=0):
    np.random.seed(seed)
    _w = jnp.asarray

    def _rec_inputs():
        import jax
        import jax.numpy as jnp
        _rk = jax.random.key(seed)
        x = -0.000125 + 0.9999 * jax.random.normal(jax.random.fold_in(_rk, 1), (128, 32, 512), jnp.float32)
        _lenS = 32 - jax.random.randint(jax.random.fold_in(_rk, 7), (128,), 0, max(1, 32 // 4) + 1, jnp.int32)
        _lenS2 = 32 - jax.random.randint(jax.random.fold_in(_rk, 8), (128,), 0, max(1, 32 // 4) + 1, jnp.int32)
        cond_128 = 0.0061147 + 1.02565 * jax.random.normal(jax.random.fold_in(_rk, 11), (128, 128), jnp.float32)
        return (x, cond_128)
    x, cond_128 = _rec_inputs()

    def _L0_cond_setup():
        import jax, jax.numpy as jnp
        import numpy as np
        K = 8
        T = 1.0
        D_EMBD = 128
        IN_C = 32
        OUT_C = 32
        BS = 32
        H = 512
        HID = 128
        key = jax.random.key(seed)
        ks = jax.random.split(key, 10)
        s = lambda fan_in: 1.0 / np.sqrt(fan_in)
        return {'x': jax.random.normal(ks[0], (BS, IN_C, H), dtype=jnp.float32), 'embedding': jax.random.normal(ks[1], (BS, D_EMBD), dtype=jnp.float32), 'W0': jax.random.normal(ks[2], (D_EMBD, HID), dtype=jnp.float32) * s(D_EMBD), 'b0': jnp.zeros((HID,), dtype=jnp.float32), 'W1': jax.random.normal(ks[3], (HID, HID), dtype=jnp.float32) * s(HID), 'b1': jnp.zeros((HID,), dtype=jnp.float32), 'W2': jax.random.normal(ks[4], (HID, K), dtype=jnp.float32) * s(HID), 'b2': jnp.zeros((K,), dtype=jnp.float32), 'weight': jax.random.normal(ks[5], (K, OUT_C, IN_C, 1), dtype=jnp.float32) * s(IN_C), 'bias_k': jax.random.normal(ks[6], (K, OUT_C), dtype=jnp.float32) * 0.1}
    _L0_cond_all = _L0_cond_setup()
    _L0_cond_in = {k: v for k, v in _L0_cond_all.items() if k in ('W0', 'b0', 'W1', 'b1', 'W2', 'b2', 'weight', 'bias_k')}
    del _L0_cond_all

    def _L0_ffn_setup():
        import jax, jax.numpy as jnp
        import numpy as np

        def sparsemax(z):
            E = z.shape[-1]
            z_sorted = -jnp.sort(-z, axis=-1)
            z_cum = jnp.cumsum(z_sorted, axis=-1)
            k = jnp.arange(1, E + 1, dtype=z.dtype)
            support = 1.0 + k * z_sorted > z_cum
            k_z = jnp.sum(support, axis=-1, keepdims=True)
            tau_sum = jnp.take_along_axis(z_cum, k_z.astype(jnp.int32) - 1, axis=-1)
            tau = (tau_sum - 1.0) / k_z.astype(z.dtype)
            return jnp.maximum(z - tau, 0.0)
        key = jax.random.key(seed)
        ks = jax.random.split(key, 6)
        B, S, D_IN, D_OUT, E, R = (8, 256, 512, 512, 8, 16)
        x = jax.random.normal(ks[0], (B, S, D_IN), dtype=jnp.float32)
        W_base = jax.random.normal(ks[1], (D_OUT, D_IN), dtype=jnp.float32) * D_IN ** (-0.5)
        b_base = jax.random.normal(ks[2], (D_OUT,), dtype=jnp.float32) * 0.01
        W_router = jax.random.normal(ks[3], (E, D_IN), dtype=jnp.float32) * D_IN ** (-0.5)
        b_router = jnp.zeros((E,), dtype=jnp.float32)
        lora_A = jax.random.normal(ks[4], (E, D_IN, R), dtype=jnp.float32) * D_IN ** (-0.5)
        lora_B = jnp.zeros((E, R, D_OUT), dtype=jnp.float32)
        return {'x': x, 'W_base': W_base, 'b_base': b_base, 'W_router': W_router, 'b_router': b_router, 'lora_A': lora_A, 'lora_B': lora_B}
    _L0_ffn_all = _L0_ffn_setup()
    _L0_ffn_in = {k: v for k, v in _L0_ffn_all.items() if k in ('W_base', 'b_base', 'W_router', 'b_router', 'lora_A', 'lora_B')}
    del _L0_ffn_all
    return {'x': x, 'cond_128': cond_128, 'L0_cond_W0': _L0_cond_in['W0'], 'L0_cond_b0': _L0_cond_in['b0'], 'L0_cond_W1': _L0_cond_in['W1'], 'L0_cond_b1': _L0_cond_in['b1'], 'L0_cond_W2': _L0_cond_in['W2'], 'L0_cond_b2': _L0_cond_in['b2'], 'L0_cond_weight': _L0_cond_in['weight'], 'L0_cond_bias_k': _L0_cond_in['bias_k'], 'L0_ffn_W_base': _L0_ffn_in['W_base'], 'L0_ffn_b_base': _L0_ffn_in['b_base'], 'L0_ffn_W_router': _L0_ffn_in['W_router'], 'L0_ffn_b_router': _L0_ffn_in['b_router'], 'L0_ffn_lora_A': _L0_ffn_in['lora_A'], 'L0_ffn_lora_B': _L0_ffn_in['lora_B']}

def reference(x, cond_128, L0_cond_W0, L0_cond_b0, L0_cond_W1, L0_cond_b1, L0_cond_W2, L0_cond_b2, L0_cond_weight, L0_cond_bias_k, L0_ffn_W_base, L0_ffn_b_base, L0_ffn_W_router, L0_ffn_b_router, L0_ffn_lora_A, L0_ffn_lora_B):
    import jax
    import jax.numpy as jnp

    def _L0_cond_ref(x, embedding, W0, b0, W1, b1, W2, b2, weight, bias_k):
        import jax, jax.numpy as jnp
        import numpy as np
        K = 8
        T = 1.0
        D_EMBD = 128
        IN_C = 32
        OUT_C = 32
        BS = 32
        H = 512
        HID = 128
        h = jax.nn.gelu(embedding @ W0 + b0, approximate=False)
        h = jax.nn.gelu(h @ W1 + b1, approximate=False)
        att = jax.nn.softmax((h @ W2 + b2) / T, axis=-1)
        agg_w = jnp.einsum('bk,koi->boi', att, weight[..., 0])
        agg_b = att @ bias_k
        out = jnp.einsum('boi,bih->boh', agg_w, x) + agg_b[:, :, None]
        return out

    def _L0_ffn_ref(x, W_base, b_base, W_router, b_router, lora_A, lora_B):
        import jax, jax.numpy as jnp
        import numpy as np

        def sparsemax(z):
            E = z.shape[-1]
            z_sorted = -jnp.sort(-z, axis=-1)
            z_cum = jnp.cumsum(z_sorted, axis=-1)
            k = jnp.arange(1, E + 1, dtype=z.dtype)
            support = 1.0 + k * z_sorted > z_cum
            k_z = jnp.sum(support, axis=-1, keepdims=True)
            tau_sum = jnp.take_along_axis(z_cum, k_z.astype(jnp.int32) - 1, axis=-1)
            tau = (tau_sum - 1.0) / k_z.astype(z.dtype)
            return jnp.maximum(z - tau, 0.0)
        base_out = jnp.einsum('bsd,od->bso', x, W_base) + b_base
        logits = jnp.einsum('bsd,ed->bse', x, W_router) + b_router
        weights = sparsemax(logits)
        h = jnp.einsum('bsd,edr->bser', x, lora_A)
        expert_out = jnp.einsum('bser,bse,ero->bso', h, weights, lora_B)
        return base_out + expert_out
    x = x + _L0_ffn_ref(_L0_cond_ref(x, cond_128, L0_cond_W0, L0_cond_b0, L0_cond_W1, L0_cond_b1, L0_cond_W2, L0_cond_b2, L0_cond_weight, L0_cond_bias_k), L0_ffn_W_base, L0_ffn_b_base, L0_ffn_W_router, L0_ffn_b_router, L0_ffn_lora_A, L0_ffn_lora_B)
    return x

_drawn_inputs = setup_inputs


def setup_inputs(seed=0):
    import zlib

    import numpy as np

    out = dict(_drawn_inputs(seed))
    spreads = {'L0_cond_b0': (0.0, 0.562),
     'L0_cond_b1': (0.0, 0.318),
     'L0_cond_b2': (0.0, 0.302),
     'L0_ffn_b_router': (0.0, 0.655),
     'L0_ffn_lora_B': (0.0, 0.1)}
    factors = {'L0_ffn_b_base': 6.151}
    for name, (base, spread) in spreads.items():
        noise = np.random.default_rng([zlib.crc32(name.encode()), seed]).standard_normal(out[name].shape)
        drawn = base * np.exp(spread * noise) if base else spread * noise
        out[name] = jnp.asarray(drawn.astype(out[name].dtype))
    for name, factor in factors.items():
        out[name] = (out[name] * factor).astype(out[name].dtype)
    return out
```

```python
from contextlib import ExitStack

import concourse.bass as bass
from concourse import mybir

F32 = mybir.dt.float32
F32R = mybir.dt.float32r
ALU = mybir.AluOpType
ACT = mybir.ActivationFunctionType
AX_X = mybir.AxisListType.X

P = 128
CH = 32
SPT = P // CH


def adaln_ffn_program(nc: bass.Bass, x, cond, wk, proj, rows, lora_b, consts, out):
    TOK, D = x.shape
    TILES = TOK // P
    C = D // P
    B = TOK // CH
    K = wk.shape[0] // 4
    HALF = proj.shape[1] // C // 2
    E = 8
    ER = lora_b.shape[0]
    R = ER // E
    BH, HH, EH = D // 2, ER // 2, E // 2
    assert HALF == BH + HH + EH and ER == P
    GB = B // 2
    GT = TILES // 2
    FIRST, LAST = 2, TILES - 2
    AHEAD = 8

    ctx = ExitStack()
    with ctx:
        def sb(name, shape, dt=F32):
            return ctx.enter_context(nc.sbuf_tensor(name, shape, dt))

        def sem(name):
            return ctx.enter_context(nc.semaphore(name))

        xs = sb("xs", [P, TILES, D])
        x_hi = sb("x_hi", [P, 2, D], F32R)
        x_lo = sb("x_lo", [P, 2, D], F32R)
        mix_hi = sb("mix_hi", [P, TILES, SPT, CH], F32R)
        mix_lo = sb("mix_lo", [P, TILES, SPT, CH], F32R)
        y_hi = sb("y_hi", [P, 2, C, P], F32R)
        y_lo = sb("y_lo", [P, 2, C, P], F32R)
        proj_raw = sb("proj_raw", [P, C, 2, HALF])
        proj_hi = sb("proj_hi", [P, C, 2, HALF], F32R)
        proj_lo = sb("proj_lo", [P, C, 2, HALF], F32R)
        lb_raw = sb("lb_raw", [P, D])
        lb_hi = sb("lb_hi", [P, D], F32R)
        lb_lo = sb("lb_lo", [P, D], F32R)
        csum = sb("csum", [P, 2, HALF])
        ones_r = sb("ones_r", [P, P], F32R)
        ones8 = sb("ones8", [P, E])
        row_sb = sb("row_sb", [P, rows.shape[1]])
        cond_sb = sb("cond_sb", [P, cond.shape[1]])
        const_sb = sb("const_sb", [P, consts.shape[1]])
        wk_raw = sb("wk_raw", [4 * K, (CH + 1) * CH])
        wk_hi = sb("wk_hi", [4 * K, (CH + 1) * CH], F32R)
        wk_rows = sb("wk_rows", [4 * K, CH + 1, CH], F32R)
        wk_st = sb("wk_st", [4 * K, CH + 1, SPT, CH], F32R)
        h0 = sb("h0", [P, B])
        h1 = sb("h1", [P, B])
        lg = sb("lg", [B, K])
        nmx = sb("nmx", [B, 1])
        ex = sb("ex", [B, K])
        esum = sb("esum", [B, 1])
        rsum = sb("rsum", [B, 1])
        att = sb("att", [B, K])
        att_hi = sb("att_hi", [B, K], F32R)
        att_st = sb("att_st", [B, 4, K])
        attT = sb("attT", [4 * K, B], F32R)
        abias = sb("abias", [P, TILES, 1])
        zb = sb("zb", [P, TILES, E])
        z = sb("z", [P, 2, E])
        zs = sb("zs", [P, 2, E])
        cs = sb("cs", [P, 2, E])
        tk = sb("tk", [P, 2, E])
        tau = sb("tau", [P, 2])
        wgt = sb("wgt", [P, 2, E])
        hb = sb("hb", [P, 2, ER])
        g = sb("g", [P, 2, ER])
        gT_hi = sb("gT_hi", [P, 2, P], F32R)
        gT_lo = sb("gT_lo", [P, 2, P], F32R)

        b_base = row_sb[:, 0:D]
        b_router = row_sb[:, D:D + E]
        b2 = row_sb[:, D + E:D + E + K]
        embT, w0, w1 = cond_sb[:, 0:B], cond_sb[:, B:B + P], cond_sb[:, B + P:B + 2 * P]
        w2 = cond_sb[:, B + 2 * P:B + 2 * P + K]
        b0 = cond_sb[:, B + 2 * P + K:B + 2 * P + K + 1]
        b1 = cond_sb[:, B + 2 * P + K + 1:B + 2 * P + K + 2]
        ident = const_sb[:, 0:P]
        neg_lo = const_sb[0:4 * K, P:P + 1]
        inv_k = const_sb[:, P + 1:P + 1 + E]

        psA = ctx.enter_context(nc.psum_tensor("psA", [P, 4, 512], F32))
        psB = ctx.enter_context(nc.psum_tensor("psB", [P, 4, 512], F32))

        def ps_y(p):
            return psA[:, p, :]

        def ps_gT(p):
            return psA[:, 2 + p, 0:P]

        def ps_out(p):
            return psB[:, 2 * p:2 * p + 2, :]

        ps_h0, ps_h1 = psB[:, 0, 0:B], psB[:, 1, 0:B]
        ps_lg, ps_attT = psB[:, 0, 128:128 + K], psB[0:4 * K, 1, 128:128 + B]
        ps_abias = psB[:, 0, 256:256 + B]
        ps_csum = psB[:, 2:4, 0:HALF]
        ps_mix = [psA, psB]

        cond_in, wk_in, rows_in, const_in, lb_in = (sem(n) for n in ("cond_in", "wk_in", "rows_in", "const_in", "lb_in"))
        proj_in = [sem(f"proj_in{c}") for c in range(C)]
        x_in = [sem("x_in_even"), sem("x_in_odd")]
        stored = sem("stored")
        ones_set, mix_zeroed = sem("ones_set"), sem("mix_zeroed")
        h0_mm, h0_done, h1_mm, h1_done, lg_mm = (sem(n) for n in ("h0_mm", "h0_done", "h1_mm", "h1_done", "lg_mm"))
        soft, exp_done, att_stacked_hi = sem("soft"), sem("exp_done"), sem("att_stacked_hi")
        att_mm, attT_done, abias_mm, abias_done = (sem(n) for n in ("att_mm", "attT_done", "abias_mm", "abias_done"))
        wk_hi_done, wk_rows_done, wk_st_done = sem("wk_hi_done"), sem("wk_rows_done"), sem("wk_st_done")
        proj_hi_done, proj_lo_done, csum_mm, csum_done = (sem(n) for n in ("proj_hi_done", "proj_lo_done", "csum_mm", "csum_done"))
        lb_hi_done, lb_lo_done = sem("lb_hi_done"), sem("lb_lo_done")
        zb_part, zb_done = sem("zb_part"), sem("zb_done")
        mixm_mm, mix_hi_done, mix_lo_done = sem("mixm_mm"), sem("mix_hi_done"), sem("mix_lo_done")
        x_hi_done, x_lo_done, xb_done, xab_done = (sem(n) for n in ("x_hi_done", "x_lo_done", "xb_done", "xab_done"))
        y_mm, y_hi_done, y_lo_done = sem("y_mm"), sem("y_hi_done"), sem("y_lo_done")
        proj_mm, g_done, gT_mm, gT_hi_done, gT_lo_done = (sem(n) for n in ("proj_mm", "g_done", "gT_mm", "gT_hi_done", "gT_lo_done"))
        out_mm, out_done = sem("out_mm"), sem("out_done")
        z_done, zs_done, cs_done, tk_done, tau_done, wgt_done, hb_done = (sem(n) for n in ("z_done", "zs_done", "cs_done", "tk_done", "tau_done", "wgt_done", "hb_done"))

        x_t = x.rearrange("(t p) d -> t p d", p=P)
        out_t = out.rearrange("(t p) d -> t p d", p=P)

        def landed(t, p):
            return (t - p) * 8 + 16

        block = ctx.enter_context(nc.Block())

        @block.sync
        def _(sp):
            def load(t, p, first=False):
                if not first:
                    sp.wait_ge(x_in[p], landed(t, p) - 16)
                sp.dma_start(xs[:, t, :], x_t[t]).then_inc(x_in[p], 16)

            def store(t):
                sp.wait_ge(out_done, t + 1)
                sp.dma_start(out_t[t], xs[:, t, :]).then_inc(stored, 16)

            sp.dma_start(cond_sb[:, :], cond).then_inc(cond_in, 16)
            sp.dma_start(wk_raw[:, :], wk).then_inc(wk_in, 16)
            load(0, 0, first=True)
            load(1, 1, first=True)
            sp.dma_start(lb_raw[:, :], lora_b).then_inc(lb_in, 16)
            with sp.Fori(2, AHEAD - 1, 2) as t:
                load(t, 0)
                load(t + 1, 1)
            with sp.Fori(0, TILES - AHEAD - 1, 2) as t:
                load(t + AHEAD, 0)
                load(t + AHEAD + 1, 1)
                store(t)
                store(t + 1)
            with sp.Fori(TILES - AHEAD, TILES) as t:
                store(t)
            sp.wait_ge(stored, 16 * TILES)

        @block.gpsimd
        def _(pool):
            nc.gpsimd.memset(ones_r[:, :].bitcast(F32), 1.0).then_inc(ones_set, 1)
            nc.gpsimd.memset(ones8[:, :], 1.0).then_inc(ones_set, 1)
            nc.gpsimd.memset(mix_hi[:, :, :, :].bitcast(F32), 0.0).then_inc(mix_zeroed, 1)
            nc.gpsimd.memset(mix_lo[:, :, :, :].bitcast(F32), 0.0).then_inc(mix_zeroed, 1)

            def split_x(t, p, first=False):
                pool.wait_ge(x_hi_done, t + 1)
                if not first:
                    pool.wait_ge(y_mm, t - 1)
                nc.gpsimd.tensor_tensor(x_lo[:, p, :], xs[:, t, :], x_hi[:, p, :].bitcast(F32),
                                        ALU.subtract).then_inc(x_lo_done, 1)
                nc.gpsimd.tensor_tensor(xs[:, t, :], xs[:, t, :], b_base, ALU.add).then_inc(xb_done, 1)

            pool.wait_ge(rows_in, 16)
            split_x(0, 0, first=True)
            split_x(1, 1, first=True)
            with pool.Fori(2, TILES - 1, 2) as t:
                split_x(t, 0)
                split_x(t + 1, 1)

        @block.scalar
        def _(act):
            act.dma_start(const_sb[:, :], consts).then_inc(const_in, 16)
            act.dma_start(row_sb[:, :], rows.broadcast_to([P, rows.shape[1]])).then_inc(rows_in, 16)
            for c in range(C):
                act.dma_start(proj_raw[:, c, :, :], proj[:, c * 2 * HALF:(c + 1) * 2 * HALF]
                              .rearrange("p (h n) -> p h n", h=2)).then_inc(proj_in[c], 16)

            def hi_x(t, p, first=False):
                act.wait_ge(x_in[p], landed(t, p))
                if not first:
                    act.wait_ge(y_mm, t - 1)
                nc.scalar.copy(x_hi[:, p, :], xs[:, t, :]).then_inc(x_hi_done, 1)

            def hi_y(t, p):
                act.wait_ge(y_mm, t + 1)
                nc.scalar.copy(y_hi[:, p, :, :], ps_y(p).rearrange("p (c n) -> p c n", c=C)).then_inc(y_hi_done, 1)

            def hi_gT(t, p):
                act.wait_ge(gT_mm, t + 1)
                nc.scalar.copy(gT_hi[:, p, :], ps_gT(p)).then_inc(gT_hi_done, 1)

            act.wait_ge(cond_in, 16)
            act.wait_ge(h0_mm, 1)
            nc.scalar.activation(h0[:, :], ps_h0, ACT.Gelu, bias=b0).then_inc(h0_done, 1)
            act.wait_ge(wk_in, 16)
            nc.scalar.copy(wk_hi[:, :], wk_raw[:, :]).then_inc(wk_hi_done, 1)
            act.wait_ge(h1_mm, 1)
            nc.scalar.activation(h1[:, :], ps_h1, ACT.Gelu, bias=b1).then_inc(h1_done, 1)
            act.wait_ge(soft, 2)
            nc.scalar.activation(ex[:, :], lg[:, :], ACT.Exp, bias=nmx[:, :],
                                 accum_out=esum[:, :]).then_inc(exp_done, 1)
            act.wait_ge(soft, 5)
            nc.scalar.copy(att_st[:, 0:2, :], att_hi[:, :].bitcast(F32).unsqueeze(1).broadcast_to([B, 2, K])
                           ).then_inc(att_stacked_hi, 1)
            hi_x(0, 0, first=True)
            hi_x(1, 1, first=True)
            for c in range(C):
                act.wait_ge(proj_in[c], 16)
                nc.scalar.copy(proj_hi[:, c, :, :], proj_raw[:, c, :, :]).then_inc(proj_hi_done, 1)
            act.wait_ge(lb_in, 16)
            nc.scalar.copy(lb_hi[:, :], lb_raw[:, :]).then_inc(lb_hi_done, 1)

            def hi_mix(half):
                act.wait_ge(mix_zeroed, 2)
                act.wait_ge(mixm_mm, half + 1)
                for s in range(SPT):
                    q = slice(CH * s, CH * s + CH)
                    src = ps_mix[half][q].rearrange("p b (o t s) -> p s t (b o)", o=8, s=SPT)[:, s]
                    nc.scalar.copy(mix_hi[q, GT * half:GT * half + GT, s, :], src).then_inc(mix_hi_done, 1)

            hi_mix(0)
            hi_mix(1)
            hi_y(0, 0)
            hi_y(1, 1)

            hi_x(2, 0)
            hi_x(3, 1)

            def step(t, p, y_more=True, x_more=True):
                if y_more:
                    hi_y(t + 2, p)
                if x_more:
                    hi_x(t + 4, p)
                hi_gT(t, p)

            with act.Fori(0, TILES - 5, 2) as t:
                step(t, 0)
                step(t + 1, 1)
            step(TILES - 4, 0, x_more=False)
            step(TILES - 3, 1, x_more=False)
            step(TILES - 2, 0, y_more=False, x_more=False)
            step(TILES - 1, 1, y_more=False, x_more=False)

        @block.vector
        def _(dve):
            dve.wait_ge(wk_hi_done, 1)
            dve.wait_ge(const_in, 16)
            nc.vector.scalar_tensor_tensor(wk_rows[:, :, :].rearrange("p o i -> p (o i)"), wk_hi[:, :].bitcast(F32),
                                           neg_lo, wk_raw[:, :], ALU.mult, ALU.add).then_inc(wk_rows_done, 1)
            dve.wait_ge(wk_rows_done, 1)
            nc.vector.tensor_copy(wk_st[:, :, :, :], wk_rows[:, :, :].unsqueeze(2).broadcast_to([4 * K, CH + 1, SPT, CH])
                                  ).then_inc(wk_st_done, 1)
            dve.wait_ge(rows_in, 16)
            dve.wait_ge(lg_mm, 1)
            nc.vector.tensor_tensor(lg[:, :], ps_lg, b2, ALU.add).then_inc(soft, 1)
            dve.wait_ge(soft, 1)
            nc.vector.tensor_reduce(nmx[:, :], lg[:, :], AX_X, ALU.max, negate=True).then_inc(soft, 1)
            dve.wait_ge(exp_done, 1)
            nc.vector.reciprocal(rsum[:, :], esum[:, :]).then_inc(soft, 1)
            dve.wait_ge(soft, 3)
            nc.vector.tensor_scalar(att[:, :], ex[:, :], rsum[:, :], None, ALU.mult).then_inc(soft, 1)
            dve.wait_ge(soft, 4)
            nc.vector.tensor_copy(att_hi[:, :], att[:, :]).then_inc(soft, 1)
            dve.wait_ge(soft, 5)
            nc.vector.tensor_tensor(att_st[:, 2:4, :], att[:, :].unsqueeze(1).broadcast_to([B, 2, K]),
                                    att_hi[:, :].bitcast(F32).unsqueeze(1).broadcast_to([B, 2, K]),
                                    ALU.subtract).then_inc(soft, 1)
            dve.wait_ge(att_mm, 1)
            nc.vector.tensor_copy(attT[:, :], ps_attT).then_inc(attT_done, 1)
            for c in range(C):
                dve.wait_ge(proj_hi_done, c + 1)
                nc.vector.tensor_tensor(proj_lo[:, c, :, :], proj_raw[:, c, :, :], proj_hi[:, c, :, :].bitcast(F32),
                                        ALU.subtract).then_inc(proj_lo_done, 1)
            dve.wait_ge(lb_hi_done, 1)
            nc.vector.tensor_tensor(lb_lo[:, :], lb_raw[:, :], lb_hi[:, :].bitcast(F32), ALU.subtract).then_inc(lb_lo_done, 1)
            dve.wait_ge(abias_mm, 1)
            for s in range(SPT):
                q = slice(CH * s, CH * s + CH)
                nc.vector.tensor_copy(abias[q, :, 0], ps_abias[q].rearrange("p (t s) -> p s t", s=SPT)[:, s]).then_inc(abias_done, 1)
            dve.wait_ge(csum_mm, 1)
            nc.vector.tensor_copy(csum[:, :, :], ps_csum).then_inc(csum_done, 1)

            def lo_mix(half):
                for s in range(SPT):
                    q = slice(CH * s, CH * s + CH)
                    dve.wait_ge(mix_hi_done, SPT * half + s + 1)
                    src = ps_mix[half][q].rearrange("p b (o t s) -> p s t (b o)", o=8, s=SPT)[:, s]
                    nc.vector.tensor_tensor(mix_lo[q, GT * half:GT * half + GT, s, :], src,
                                            mix_hi[q, GT * half:GT * half + GT, s, :].bitcast(F32),
                                            ALU.subtract).then_inc(mix_lo_done, 1)

            lo_mix(0)
            lo_mix(1)
            dve.wait_ge(abias_done, SPT)
            dve.wait_ge(csum_done, 1)
            for h in range(2):
                zh = zb[:, :, EH * h:EH * h + EH]
                nc.vector.tensor_tensor(zh, abias[:, :, :].broadcast_to([P, TILES, EH]),
                                        csum[:, h, BH + HH:HALF].unsqueeze(1).broadcast_to([P, TILES, EH]),
                                        ALU.mult).then_inc(zb_part, 1)
            dve.wait_ge(zb_part, 2)
            nc.vector.tensor_tensor(zb[:, :, :], zb[:, :, :], b_router.unsqueeze(1).broadcast_to([P, TILES, E]),
                                    ALU.add).then_inc(zb_done, 1)

            def lo_y(t, p):
                dve.wait_ge(y_hi_done, t + 1)
                nc.vector.tensor_tensor(y_lo[:, p, :, :], ps_y(p).rearrange("p (c n) -> p c n", c=C),
                                        y_hi[:, p, :, :].bitcast(F32), ALU.subtract).then_inc(y_lo_done, 1)

            lo_y(0, 0)
            lo_y(1, 1)
            dve.wait_ge(zb_done, 1)
            dve.wait_ge(ones_set, 2)

            def route(t, p):
                ps = ps_out(p)
                dve.wait_ge(proj_mm, t + 1)
                nc.vector.tensor_tensor(z[:, p, :].rearrange("p (h e) -> p h e", h=2), ps[:, :, BH + HH:HALF],
                                        zb[:, t, :].rearrange("p (h e) -> p h e", h=2), ALU.add).then_inc(z_done, 1)
                dve.wait_ge(z_done, t + 1)
                nc.vector.scalar_tensor_tensor(hb[:, p, :].rearrange("p (h n) -> p h n", h=2), csum[:, :, BH:BH + HH],
                                               abias[:, t, :], ps[:, :, BH:BH + HH],
                                               ALU.mult, ALU.add).then_inc(hb_done, 1)
                nc.vector.max(zs[:, p, :], z[:, p, :]).then_inc(zs_done, 1)
                dve.wait_ge(zs_done, t + 1)
                nc.vector.tensor_tensor_scan(cs[:, p, :], ones8[:, :], zs[:, p, :], -1.0, ALU.mult, ALU.add).then_inc(cs_done, 1)
                dve.wait_ge(cs_done, t + 1)
                nc.vector.tensor_tensor(tk[:, p, :], cs[:, p, :], inv_k, ALU.mult).then_inc(tk_done, 1)
                dve.wait_ge(tk_done, t + 1)
                nc.vector.tensor_reduce(tau[:, p:p + 1], tk[:, p, :], AX_X, ALU.max).then_inc(tau_done, 1)
                dve.wait_ge(tau_done, t + 1)
                nc.vector.tensor_scalar(wgt[:, p, :], z[:, p, :], tau[:, p:p + 1], 0.0,
                                        ALU.subtract, ALU.max).then_inc(wgt_done, 1)
                dve.wait_ge(hb_done, t + 1)
                dve.wait_ge(wgt_done, t + 1)
                nc.vector.tensor_tensor(g[:, p, :].rearrange("p (e r) -> p e r", e=E),
                                        hb[:, p, :].rearrange("p (e r) -> p e r", e=E),
                                        wgt[:, p, :].unsqueeze(2).broadcast_to([P, E, R]), ALU.mult).then_inc(g_done, 1)

            def lo_gT(t, p):
                dve.wait_ge(gT_hi_done, t + 1)
                nc.vector.tensor_tensor(gT_lo[:, p, :], ps_gT(p), gT_hi[:, p, :].bitcast(F32),
                                        ALU.subtract).then_inc(gT_lo_done, 1)

            def residual(t):
                dve.wait_ge(xb_done, t + 1)
                nc.vector.scalar_tensor_tensor(xs[:, t, :].rearrange("p (h n) -> p h n", h=2), csum[:, :, 0:BH],
                                               abias[:, t, :], xs[:, t, :].rearrange("p (h n) -> p h n", h=2),
                                               ALU.mult, ALU.add).then_inc(xab_done, 1)

            def finish(t, p):
                dve.wait_ge(xab_done, t + 1)
                dve.wait_ge(out_mm, t + 1)
                nc.vector.tensor_tensor(xs[:, t, :].rearrange("p (h n) -> p h n", h=2), ps_out(p)[:, :, 0:BH],
                                        xs[:, t, :].rearrange("p (h n) -> p h n", h=2), ALU.add).then_inc(out_done, 1)

            def step(t, p, y_more=True):
                route(t, p)
                if y_more:
                    lo_y(t + 2, p)
                residual(t)
                lo_gT(t, p)
                finish(t, p)

            with dve.Fori(0, LAST - 1, 2) as t:
                step(t, 0)
                step(t + 1, 1)
            step(LAST, 0, y_more=False)
            step(LAST + 1, 1, y_more=False)

        @block.tensor
        def _(pe):
            pe.wait_ge(cond_in, 16)
            nc.tensor.matmul(ps_h0, w0, embT, start=True, stop=True).then_inc(h0_mm, 1)
            pe.wait_ge(h0_done, 1)
            nc.tensor.matmul(ps_h1, w1, h0[:, :], start=True, stop=True).then_inc(h1_mm, 1)
            pe.wait_ge(h1_done, 1)
            nc.tensor.matmul(ps_lg, h1[:, :], w2, start=True, stop=True).then_inc(lg_mm, 1)
            pe.wait_ge(att_stacked_hi, 1)
            pe.wait_ge(soft, 6)
            pe.wait_ge(const_in, 16)
            nc.tensor.transpose(ps_attT, att_st[:, :, :].rearrange("b c k -> b (c k)"), ident).then_inc(att_mm, 1)
            pe.wait_ge(attT_done, 1)
            pe.wait_ge(wk_st_done, 1)

            def mix_matrices(half):
                for o in range(CH):
                    mm = nc.tensor.matmul(ps_mix[half][:, o // 8, (o % 8) * GB:(o % 8) * GB + GB],
                                          wk_st[:, o, :, :].rearrange("p s i -> p (s i)"),
                                          attT[:, GB * half:GB * half + GB], start=True, stop=True)
                mm.then_inc(mixm_mm, 1)

            mix_matrices(0)
            nc.tensor.matmul(ps_abias, wk_st[:, CH, :, :].rearrange("p s i -> p (s i)"),
                             attT[:, :], start=True, stop=True).then_inc(abias_mm, 1)
            pe.wait_ge(ones_set, 2)
            for c in range(C):
                pe.wait_ge(proj_lo_done, c + 1)
                for part in (proj_hi, proj_lo):
                    for h in range(2):
                        mm = nc.tensor.matmul(ps_csum[:, h, :], ones_r[:, :], part[:, c, h, :],
                                              start=(c == 0 and part is proj_hi), stop=(c == C - 1 and part is proj_lo))
            mm.then_inc(csum_mm, 1)
            pe.wait_ge(abias_done, SPT)
            pe.wait_ge(csum_done, 1)
            mix_matrices(1)

            def mix(t, p):
                pe.wait_ge(x_lo_done, t + 1)
                for c in range(C):
                    o = ps_y(p)[:, c * P:(c + 1) * P]
                    xh, xl = x_hi[:, p, c * P:(c + 1) * P], x_lo[:, p, c * P:(c + 1) * P]
                    ah = mix_hi[:, t, :, :].rearrange("p s o -> p (s o)")
                    al = mix_lo[:, t, :, :].rearrange("p s o -> p (s o)")
                    nc.tensor.matmul(o, xh, ah, start=True, stop=False)
                    nc.tensor.matmul(o, xh, al, start=False, stop=False)
                    mm = nc.tensor.matmul(o, xl, ah, start=False, stop=True)
                mm.then_inc(y_mm, 1)

            def project(p, chunks):
                for c in chunks:
                    for n, (a, b) in enumerate(((y_hi, proj_hi), (y_hi, proj_lo), (y_lo, proj_hi))):
                        for h in range(2):
                            mm = nc.tensor.matmul(ps_out(p)[:, h, 0:HALF], a[:, p, c, :], b[:, c, h, :],
                                                  start=(c == 0 and n == 0), stop=(c == C - 1 and n == 2))
                return mm

            def transpose_g(t, p):
                pe.wait_ge(g_done, t + 1)
                nc.tensor.transpose(ps_gT(p), g[:, p, :], ident).then_inc(gT_mm, 1)

            def lora_out(t, p):
                pe.wait_ge(gT_lo_done, t + 1)
                for n, (a, b) in enumerate(((gT_hi, lb_hi), (gT_hi, lb_lo), (gT_lo, lb_hi))):
                    for h in range(2):
                        mm = nc.tensor.matmul(ps_out(p)[:, h, 0:BH], a[:, p, :], b[:, h * BH:(h + 1) * BH],
                                              start=False, stop=(n == 2), skip_group_check=True)
                mm.then_inc(out_mm, 1)

            def step(t, p, before=True, more=True):
                pe.wait_ge(y_lo_done, t + 1)
                if before == "far":
                    pe.wait_ge(out_done, t - 1)
                project(p, range(0, 2))
                if before:
                    transpose_g(t - 1, 1 - p)
                project(p, range(2, 3))
                if before:
                    lora_out(t - 1, 1 - p)
                project(p, range(3, C)).then_inc(proj_mm, 1)
                if more:
                    mix(t + 2, p)

            pe.wait_ge(mix_lo_done, SPT)
            mix(0, 0)
            mix(1, 1)
            pe.wait_ge(mix_lo_done, 2 * SPT)
            pe.wait_ge(lb_lo_done, 1)
            step(0, 0, before=False)
            step(1, 1)
            with pe.Fori(FIRST, LAST - 1, 2) as t:
                step(t, 0, before="far")
                step(t + 1, 1, before="far")
            step(LAST, 0, before="far", more=False)
            step(LAST + 1, 1, before="far", more=False)
            transpose_g(LAST + 1, 1)
            lora_out(LAST + 1, 1)


def kernel(x, cond_128, L0_cond_W0, L0_cond_b0, L0_cond_W1, L0_cond_b1, L0_cond_W2, L0_cond_b2, L0_cond_weight,
           L0_cond_bias_k, L0_ffn_W_base, L0_ffn_b_base, L0_ffn_W_router, L0_ffn_b_router, L0_ffn_lora_A,
           L0_ffn_lora_B):
    import numpy as np
    import concourse.bacc as bacc
    from concourse.bass_utils import run_bass_kernel_spmd

    x = np.asarray(x)
    S, ch, D = x.shape
    E, _, R = L0_ffn_lora_A.shape
    K = L0_cond_W2.shape[1]
    wbT = np.asarray(L0_ffn_W_base).T.reshape(D, 2, D // 2)
    la = np.asarray(L0_ffn_lora_A).transpose(1, 0, 2).reshape(D, 2, E * R // 2)
    wrT = np.asarray(L0_ffn_W_router).T.reshape(D, 2, E // 2)
    proj = np.concatenate([wbT, la, wrT], axis=2).reshape(D // 128, 128, -1).transpose(1, 0, 2).reshape(128, -1)
    cond = np.concatenate([np.asarray(cond_128).T, np.asarray(L0_cond_W0), np.asarray(L0_cond_W1),
                           np.asarray(L0_cond_W2), np.asarray(L0_cond_b0)[:, None],
                           np.asarray(L0_cond_b1)[:, None]], axis=1)
    wk = np.concatenate([np.asarray(L0_cond_weight).reshape(K, -1), np.asarray(L0_cond_bias_k)], axis=1)
    wk = np.concatenate([wk] * 4, axis=0)
    rows = np.concatenate([np.asarray(L0_ffn_b_base), np.asarray(L0_ffn_b_router), np.asarray(L0_cond_b2)])[None]
    lora_b = np.asarray(L0_ffn_lora_B).reshape(E * R, D)
    consts = np.zeros((128, 128 + 1 + E), np.float32)
    consts[:, :128] = np.eye(128, dtype=np.float32)
    for c in (1, 3):
        consts[c * K:(c + 1) * K, 128] = -1.0
    consts[:, 129:] = np.float32(1.0) / np.arange(1, E + 1, dtype=np.float32)

    arrays = {"x_in_dram": x.reshape(S * ch, D), "cond_dram": cond, "wk_dram": wk, "proj_dram": proj,
              "rows_dram": rows, "lora_b_dram": lora_b, "consts_dram": consts}
    arrays = {n: np.ascontiguousarray(a) for n, a in arrays.items()}
    nc = bacc.Bacc("TRN2", target_bir_lowering=False, num_devices=1)
    args = [nc.dram_tensor(n, a.shape, mybir.dt.from_np(a.dtype), kind="ExternalInput").ap() for n, a in arrays.items()]
    args.append(nc.dram_tensor("out_dram", (S * ch, D), F32, kind="ExternalOutput").ap())
    adaln_ffn_program(nc, *args)
    r = run_bass_kernel_spmd(nc, [arrays], core_ids=[0])
    return r.results[0]["out_dram"].reshape(S, ch, D)
```

```python
from contextlib import ExitStack

import concourse.bass as bass
from concourse import mybir

F32 = mybir.dt.float32
F32R = mybir.dt.float32r
ALU = mybir.AluOpType
ACT = mybir.ActivationFunctionType
AX_X = mybir.AxisListType.X

P = 128
CH = 32
SPT = P // CH


def adaln_ffn_program(nc: bass.Bass, x, cond, wk, proj, b_row, lora_b, consts, out):
    TOK, D = x.shape
    TILES = TOK // P
    C = D // P
    B = TOK // CH
    K = wk.shape[0] // 4
    HALF = proj.shape[1] // C // 2
    E = 8
    ER = lora_b.shape[0]
    R = ER // E
    BH, HH, EH = D // 2, ER // 2, E // 2
    assert HALF == BH + HH + EH and ER == P
    OG = P // CH
    NG = CH // OG
    EARLY = 8
    FIRST, LAST = 2, TILES - 2
    AHEAD = 8

    ctx = ExitStack()
    with ctx:
        def sb(name, shape, dt=F32):
            return ctx.enter_context(nc.sbuf_tensor(name, shape, dt))

        def sem(name):
            return ctx.enter_context(nc.semaphore(name))

        xs = sb("xs", [P, TILES, D])
        x_hi = sb("x_hi", [P, 2, D], F32R)
        x_lo = sb("x_lo", [P, 2, D], F32R)
        agg = sb("agg", [P, TILES, 2, CH], F32R)
        agg_f = sb("agg_f", [P, TILES, CH])
        mixm = sb("mixm", [P, 2, 2, SPT, CH], F32R)
        y_hi = sb("y_hi", [P, 2, C, P], F32R)
        y_lo = sb("y_lo", [P, 2, C, P], F32R)
        y_tmp = sb("y_tmp", [P, C, P])
        proj_raw = sb("proj_raw", [P, C, 2, HALF])
        proj_hi = sb("proj_hi", [P, C, 2, HALF], F32R)
        proj_lo = sb("proj_lo", [P, C, 2, HALF], F32R)
        lb_raw = sb("lb_raw", [P, D])
        lb_hi = sb("lb_hi", [P, D], F32R)
        lb_lo = sb("lb_lo", [P, D], F32R)
        csum = sb("csum", [P, 2, HALF])
        ones_r = sb("ones_r", [P, P], F32R)
        ones8 = sb("ones8", [P, E])
        b_base = sb("b_base", [P, D])
        ab_row = sb("ab_row", [P, 2, D])
        warm = sb("warm", [P, 1])
        cond_sb = sb("cond_sb", [P, cond.shape[1]])
        const_sb = sb("const_sb", [P, consts.shape[1]])
        wk_raw = sb("wk_raw", [4 * K, wk.shape[1]])
        wk_hi = sb("wk_hi", [4 * K, wk.shape[1]], F32R)
        wk_st = sb("wk_st", [4 * K, wk.shape[1]], F32R)
        h0 = sb("h0", [P, B])
        h1 = sb("h1", [P, B])
        lg = sb("lg", [B, K])
        nmx = sb("nmx", [B, 1])
        ex = sb("ex", [B, K])
        esum = sb("esum", [B, 1])
        rsum = sb("rsum", [B, 1])
        att = sb("att", [B, K])
        att_hi = sb("att_hi", [B, K], F32R)
        att_st = sb("att_st", [B, 4, K])
        attT = sb("attT", [4 * K, B], F32R)
        abias = sb("abias", [P, TILES, 1])
        zb = sb("zb", [P, TILES, E])
        z = sb("z", [P, 2, E])
        zs = sb("zs", [P, 2, E])
        cs = sb("cs", [P, 2, E])
        tk = sb("tk", [P, 2, E])
        tau = sb("tau", [P, 2])
        wgt = sb("wgt", [P, 2, E])
        hb = sb("hb", [P, 2, ER])
        g = sb("g", [P, 2, ER])
        gT_hi = sb("gT_hi", [P, 2, P], F32R)
        gT_lo = sb("gT_lo", [P, 2, P], F32R)

        at = 0

        def columns(n, tile):
            nonlocal at
            at += n
            return tile[:, at - n:at]

        embT, w0, w1, w2, b2, b_router, b0, b1 = (columns(n, cond_sb) for n in (B, P, P, K, K, E, 1, 1))
        at = 0
        ident, inv_k, neg_lo = (columns(n, const_sb) for n in (P, E, 1))

        psA = ctx.enter_context(nc.psum_tensor("psA", [P, 4, 512], F32))
        psB = ctx.enter_context(nc.psum_tensor("psB", [P, 4, 512], F32))

        ps_y = psA[:, 0:2, :].rearrange("p b (c m n) -> p (b c) m n", c=C // 2, m=2)

        def ps_gT(p):
            return psA[:, 2 + p, 0:P]

        def ps_out(p):
            return psB[:, 2 * p:2 * p + 2, :]

        ps_h0, ps_h1, ps_lg = psA[:, 2, 0:B], psA[:, 3, 0:B], psA[:, 2, 128:128 + K]
        ps_attT, ps_abias = psA[0:4 * K, 3, 128:128 + B], psA[:, 2, 256:256 + B]
        ps_csum = psB[:, 0:2, 0:HALF]
        ps_agg = psB[:, 2:4, :].rearrange("p c (g b) -> p (c g) b", b=B)

        cond_in, wk_in, b_row_in, const_in, lb_in = (sem(n) for n in ("cond_in", "wk_in", "b_row_in", "const_in", "lb_in"))
        proj_in = [sem(f"proj_in{c}") for c in range(C)]
        warm_set, exp_loaded = sem("warm_set"), sem("exp_loaded")
        x_in = [sem("x_in_even"), sem("x_in_odd")]
        stored = sem("stored")
        ones_set = sem("ones_set")
        h0_mm, h0_done, h1_mm, h1_done, lg_mm = (sem(n) for n in ("h0_mm", "h0_done", "h1_mm", "h1_done", "lg_mm"))
        soft, exp_done, att_stacked = sem("soft"), sem("exp_done"), sem("att_stacked")
        att_mm, attT_done, abias_mm, abias_done = (sem(n) for n in ("att_mm", "attT_done", "abias_mm", "abias_done"))
        wk_hi_done, wk_st_done = sem("wk_hi_done"), sem("wk_st_done")
        mixm_zeroed, agg_f_act, agg_f_dve = sem("mixm_zeroed"), sem("agg_f_act"), sem("agg_f_dve")
        proj_hi_done, csum_mm, csum_done = (sem(n) for n in ("proj_hi_done", "csum_mm", "csum_done"))
        proj_lo_done = [sem(f"proj_lo_done{c}") for c in range(C)]
        lb_hi_done, lb_lo_done = sem("lb_hi_done"), sem("lb_lo_done")
        zb_part, zb_done = sem("zb_part"), sem("zb_done")
        agg_mm, agg_hi_done, agg_lo_done = sem("agg_mm"), sem("agg_hi_done"), sem("agg_lo_done")
        x_hi_done, x_lo_done, xb_done, xab_done = (sem(n) for n in ("x_hi_done", "x_lo_done", "xb_done", "xab_done"))
        mixm_done, ab_row_done, y_tmp_done = sem("mixm_done"), sem("ab_row_done"), sem("y_tmp_done")
        y_mm, y_hi_done, y_lo_done = sem("y_mm"), sem("y_hi_done"), sem("y_lo_done")
        proj_mm, g_done, gT_mm, gT_hi_done, gT_lo_done = (sem(n) for n in ("proj_mm", "g_done", "gT_mm", "gT_hi_done", "gT_lo_done"))
        out_mm, out_done = sem("out_mm"), sem("out_done")
        z_done, zs_done, cs_done, tk_done, tau_done, wgt_done, hb_done = (sem(n) for n in ("z_done", "zs_done", "cs_done", "tk_done", "tau_done", "wgt_done", "hb_done"))

        x_t = x.rearrange("(t p) d -> t p d", p=P)
        out_t = out.rearrange("(t p) d -> t p d", p=P)

        def landed(t, p):
            return (t - p) * 8 + 16

        block = ctx.enter_context(nc.Block())

        @block.sync
        def _(sp):
            def load(t, p, first=False):
                if not first:
                    sp.wait_ge(x_in[p], landed(t, p) - 16)
                sp.dma_start(xs[:, t, :], x_t[t]).then_inc(x_in[p], 16)

            def store(t):
                sp.wait_ge(out_done, t + 1)
                sp.dma_start(out_t[t], xs[:, t, :]).then_inc(stored, 16)

            sp.dma_start(cond_sb[:, :], cond).then_inc(cond_in, 16)
            sp.dma_start(wk_raw[:, :], wk).then_inc(wk_in, 16)
            sp.dma_start(const_sb[:, :], consts).then_inc(const_in, 16)
            load(0, 0, first=True)
            for c in range(C):
                sp.dma_start(proj_raw[:, c, :, :], proj[:, c * 2 * HALF:(c + 1) * 2 * HALF]
                             .rearrange("p (h n) -> p h n", h=2)).then_inc(proj_in[c], 16)
            load(1, 1, first=True)
            sp.dma_start(lb_raw[:, :], lora_b).then_inc(lb_in, 16)
            sp.dma_start(b_base[:, :], b_row.broadcast_to([P, D])).then_inc(b_row_in, 16)
            with sp.Fori(2, AHEAD - 1, 2) as t:
                load(t, 0)
                load(t + 1, 1)
            with sp.Fori(0, TILES - AHEAD - 1, 2) as t:
                load(t + AHEAD, 0)
                load(t + AHEAD + 1, 1)
                store(t)
                store(t + 1)
            with sp.Fori(TILES - AHEAD, TILES) as t:
                store(t)
            sp.wait_ge(stored, 16 * TILES)

        @block.gpsimd
        def _(pool):
            nc.gpsimd.memset(warm[:, :], 0.0).then_inc(warm_set, 1)
            nc.gpsimd.memset(ones_r[:, :].bitcast(F32), 1.0).then_inc(ones_set, 1)
            nc.gpsimd.memset(ones8[:, :], 1.0).then_inc(ones_set, 1)
            nc.gpsimd.memset(mixm[:, :, :, :, :].bitcast(F32), 0.0).then_inc(mixm_zeroed, 1)

            def lo_x(t, p):
                nc.gpsimd.tensor_tensor(x_lo[:, p, :], xs[:, t, :], x_hi[:, p, :].bitcast(F32),
                                        ALU.subtract).then_inc(x_lo_done, 1)

            def residual(t, p):
                nc.gpsimd.tensor_tensor(xs[:, t, :], xs[:, t, :], ab_row[:, p, :], ALU.add).then_inc(xb_done, 1)
                pool.wait_ge(b_row_in, 16)
                pool.wait_ge(xb_done, t + 1)
                nc.gpsimd.tensor_tensor(xs[:, t, :], xs[:, t, :], b_base[:, :], ALU.add).then_inc(xab_done, 1)

            def split_and_add(t, p):
                pool.wait_ge(x_hi_done, t + 1)
                pool.wait_ge(y_mm, t - 1)
                pool.wait_ge(ab_row_done, t + 1)
                lo_x(t, p)
                residual(t, p)

            pool.wait_ge(x_hi_done, 1)
            lo_x(0, 0)
            pool.wait_ge(proj_hi_done, C)
            nc.gpsimd.tensor_tensor(proj_lo[:, C - 1, :, :], proj_raw[:, C - 1, :, :],
                                    proj_hi[:, C - 1, :, :].bitcast(F32), ALU.subtract).then_inc(proj_lo_done[C - 1], 1)
            pool.wait_ge(x_hi_done, 2)
            lo_x(1, 1)
            pool.wait_ge(lb_hi_done, 1)
            nc.gpsimd.tensor_tensor(lb_lo[:, :], lb_raw[:, :], lb_hi[:, :].bitcast(F32), ALU.subtract).then_inc(lb_lo_done, 1)
            pool.wait_ge(ab_row_done, 1)
            residual(0, 0)
            pool.wait_ge(ab_row_done, 2)
            residual(1, 1)
            with pool.Fori(2, TILES - 1, 2) as t:
                split_and_add(t, 0)
                split_and_add(t + 1, 1)

        @block.scalar
        def _(act):
            def hi_x(t, p, first=False):
                act.wait_ge(x_in[p], landed(t, p))
                if not first:
                    act.wait_ge(y_mm, t - 1)
                nc.scalar.copy(x_hi[:, p, :], xs[:, t, :]).then_inc(x_hi_done, 1)

            def hi_y(t, p):
                act.wait_ge(y_mm, t + 1)
                nc.scalar.copy(y_hi[:, p, :, :], ps_y[:, :, 0, :]).then_inc(y_hi_done, 1)

            def spread_mix(t, p, first=False):
                if not first:
                    act.wait_ge(y_mm, t - 1)
                for s in range(SPT):
                    q = slice(CH * s, CH * s + CH)
                    cp = nc.scalar.copy(mixm[q, p, :, s, :], agg[q, t, :, :].bitcast(F32))
                cp.then_inc(mixm_done, 1)

            def scale_csum(t, p, first=False):
                if not first:
                    act.wait_ge(xab_done, t - 1)
                nc.scalar.activation(ab_row[:, p, :].rearrange("p (h n) -> p h n", h=2), csum[:, :, 0:BH],
                                     ACT.Copy, scale=abias[:, t, :]).then_inc(ab_row_done, 1)

            def hi_gT(t, p):
                act.wait_ge(gT_mm, t + 1)
                nc.scalar.copy(gT_hi[:, p, :], ps_gT(p)).then_inc(gT_hi_done, 1)

            act.wait_ge(warm_set, 1)
            nc.scalar.activation(warm[:, :], warm[:, :], ACT.Gelu).then_inc(exp_loaded, 1)
            act.wait_ge(cond_in, 16)
            act.wait_ge(h0_mm, 1)
            nc.scalar.activation(h0[:, :], ps_h0, ACT.Gelu, bias=b0).then_inc(h0_done, 1)
            act.wait_ge(h1_mm, 1)
            nc.scalar.activation(h1[:, :], ps_h1, ACT.Gelu, bias=b1).then_inc(h1_done, 1)
            act.wait_ge(exp_loaded, 1)
            nc.scalar.activation(warm[:, :], warm[:, :], ACT.Exp).then_inc(exp_loaded, 1)
            act.wait_ge(soft, 2)
            nc.scalar.activation(ex[:, :], lg[:, :], ACT.Exp, bias=nmx[:, :],
                                 accum_out=esum[:, :]).then_inc(exp_done, 1)
            hi_x(0, 0, first=True)

            def lay_out_agg(tiles):
                for j in range(OG // 2):
                    for s in range(SPT):
                        cp = nc.scalar.copy(agg_f[CH * s:CH * s + CH, tiles, :].rearrange("p t (g j) -> p j t g", j=OG)[:, j],
                                            ps_agg[CH * j:CH * j + CH].rearrange("p g (t s) -> p s t g", s=SPT)[:, s, tiles])
                cp.then_inc(agg_f_act, 1)

            def hi_agg(tiles, n):
                act.wait_ge(agg_f_act, n)
                act.wait_ge(agg_f_dve, n)
                nc.scalar.copy(agg[:, tiles, 0, :], agg_f[:, tiles, :]).then_inc(agg_hi_done, 1)

            act.wait_ge(agg_mm, 1)
            lay_out_agg(slice(0, EARLY))
            hi_agg(slice(0, EARLY), 1)
            act.wait_ge(mixm_zeroed, 1)
            act.wait_ge(agg_lo_done, 1)
            spread_mix(0, 0, first=True)
            spread_mix(1, 1, first=True)
            for c in range(C):
                act.wait_ge(proj_in[c], 16)
                nc.scalar.copy(proj_hi[:, c, :, :], proj_raw[:, c, :, :]).then_inc(proj_hi_done, 1)
            hi_x(1, 1, first=True)
            lay_out_agg(slice(EARLY, TILES))
            hi_agg(slice(EARLY, TILES), 2)
            act.wait_ge(lb_in, 16)
            nc.scalar.copy(lb_hi[:, :], lb_raw[:, :]).then_inc(lb_hi_done, 1)
            hi_y(0, 0)
            hi_y(1, 1)
            act.wait_ge(csum_done, 1)
            act.wait_ge(abias_done, SPT)
            scale_csum(0, 0, first=True)
            scale_csum(1, 1, first=True)
            hi_x(2, 0)
            scale_csum(2, 0)
            hi_x(3, 1)
            scale_csum(3, 1)
            spread_mix(2, 0)
            spread_mix(3, 1)
            act.wait_ge(agg_lo_done, 2)

            def step(t, p, y_more=True, x_more=True):
                if y_more:
                    hi_y(t + 2, p)
                if x_more:
                    hi_x(t + 4, p)
                    scale_csum(t + 4, p)
                hi_gT(t, p)
                if x_more:
                    spread_mix(t + 4, p)

            with act.Fori(0, TILES - 5, 2) as t:
                step(t, 0)
                step(t + 1, 1)
            step(TILES - 4, 0, x_more=False)
            step(TILES - 3, 1, x_more=False)
            step(TILES - 2, 0, y_more=False, x_more=False)
            step(TILES - 1, 1, y_more=False, x_more=False)

        @block.vector
        def _(dve):
            dve.wait_ge(wk_in, 16)
            nc.vector.tensor_copy(wk_hi[:, :], wk_raw[:, :]).then_inc(wk_hi_done, 1)
            dve.wait_ge(wk_hi_done, 1)
            dve.wait_ge(const_in, 16)
            nc.vector.scalar_tensor_tensor(wk_st[:, :], wk_hi[:, :].bitcast(F32), neg_lo[0:4 * K], wk_raw[:, :],
                                           ALU.mult, ALU.add).then_inc(wk_st_done, 1)
            dve.wait_ge(lg_mm, 1)
            nc.vector.tensor_tensor(lg[:, :], ps_lg, b2, ALU.add).then_inc(soft, 1)
            dve.wait_ge(soft, 1)
            nc.vector.tensor_reduce(nmx[:, :], lg[:, :], AX_X, ALU.max, negate=True).then_inc(soft, 1)
            dve.wait_ge(exp_done, 1)
            nc.vector.reciprocal(rsum[:, :], esum[:, :]).then_inc(soft, 1)
            dve.wait_ge(soft, 3)
            nc.vector.tensor_scalar(att[:, :], ex[:, :], rsum[:, :], None, ALU.mult).then_inc(soft, 1)
            dve.wait_ge(soft, 4)
            nc.vector.tensor_copy(att_hi[:, :], att[:, :]).then_inc(soft, 1)
            dve.wait_ge(soft, 5)
            nc.vector.tensor_copy(att_st[:, 0:2, :], att_hi[:, :].bitcast(F32).unsqueeze(1).broadcast_to([B, 2, K])
                                  ).then_inc(att_stacked, 1)
            nc.vector.tensor_tensor(att_st[:, 2:4, :], att[:, :].unsqueeze(1).broadcast_to([B, 2, K]),
                                    att_hi[:, :].bitcast(F32).unsqueeze(1).broadcast_to([B, 2, K]),
                                    ALU.subtract).then_inc(att_stacked, 1)
            dve.wait_ge(att_mm, 1)
            nc.vector.tensor_copy(attT[:, :], ps_attT).then_inc(attT_done, 1)

            def lay_out_agg(tiles):
                for j in range(OG // 2, OG):
                    for s in range(SPT):
                        cp = nc.vector.tensor_copy(agg_f[CH * s:CH * s + CH, tiles, :].rearrange("p t (g j) -> p j t g", j=OG)[:, j],
                                                   ps_agg[CH * j:CH * j + CH].rearrange("p g (t s) -> p s t g", s=SPT)[:, s, tiles])
                cp.then_inc(agg_f_dve, 1)

            def lo_agg(tiles, n):
                dve.wait_ge(agg_hi_done, n)
                nc.vector.tensor_tensor(agg[:, tiles, 1, :], agg_f[:, tiles, :], agg[:, tiles, 0, :].bitcast(F32),
                                        ALU.subtract).then_inc(agg_lo_done, 1)

            dve.wait_ge(agg_mm, 1)
            lay_out_agg(slice(0, EARLY))
            lo_agg(slice(0, EARLY), 1)
            dve.wait_ge(abias_mm, 1)
            for s in range(SPT):
                q = slice(CH * s, CH * s + CH)
                nc.vector.tensor_copy(abias[q, :, 0], ps_abias[q].rearrange("p (t s) -> p s t", s=SPT)[:, s]).then_inc(abias_done, 1)
            for c in range(C - 1):
                dve.wait_ge(proj_hi_done, c + 1)
                nc.vector.tensor_tensor(proj_lo[:, c, :, :], proj_raw[:, c, :, :], proj_hi[:, c, :, :].bitcast(F32),
                                        ALU.subtract).then_inc(proj_lo_done[c], 1)

            def lo_y(t, p, part):
                if part == 0:
                    dve.wait_ge(y_hi_done, t + 1)
                    nc.vector.tensor_tensor(y_tmp[:, :, :], ps_y[:, :, 0, :], y_hi[:, p, :, :].bitcast(F32),
                                            ALU.subtract).then_inc(y_tmp_done, 1)
                else:
                    dve.wait_ge(y_tmp_done, t + 1)
                    nc.vector.tensor_tensor(y_lo[:, p, :, :], ps_y[:, :, 1, :], y_tmp[:, :, :], ALU.add).then_inc(y_lo_done, 1)

            lay_out_agg(slice(EARLY, TILES))
            lo_y(0, 0, 0)
            lo_y(0, 0, 1)
            dve.wait_ge(csum_mm, 1)
            nc.vector.tensor_copy(csum[:, :, :], ps_csum).then_inc(csum_done, 1)
            lo_agg(slice(EARLY, TILES), 2)
            lo_y(1, 1, 0)
            lo_y(1, 1, 1)
            dve.wait_ge(abias_done, SPT)
            dve.wait_ge(csum_done, 1)
            for h in range(2):
                zh = zb[:, :, EH * h:EH * h + EH]
                nc.vector.tensor_tensor(zh, abias[:, :, :].broadcast_to([P, TILES, EH]),
                                        csum[:, h, BH + HH:HALF].unsqueeze(1).broadcast_to([P, TILES, EH]),
                                        ALU.mult).then_inc(zb_part, 1)
            dve.wait_ge(zb_part, 2)
            nc.vector.tensor_tensor(zb[:, :, :], zb[:, :, :], b_router.unsqueeze(1).broadcast_to([P, TILES, E]),
                                    ALU.add).then_inc(zb_done, 1)
            dve.wait_ge(zb_done, 1)
            dve.wait_ge(ones_set, 2)

            def route(t, p):
                ps = ps_out(p)
                dve.wait_ge(proj_mm, t + 1)
                nc.vector.tensor_tensor(z[:, p, :].rearrange("p (h e) -> p h e", h=2), ps[:, :, BH + HH:HALF],
                                        zb[:, t, :].rearrange("p (h e) -> p h e", h=2), ALU.add).then_inc(z_done, 1)
                dve.wait_ge(z_done, t + 1)
                nc.vector.scalar_tensor_tensor(hb[:, p, :].rearrange("p (h n) -> p h n", h=2), csum[:, :, BH:BH + HH],
                                               abias[:, t, :], ps[:, :, BH:BH + HH],
                                               ALU.mult, ALU.add).then_inc(hb_done, 1)
                nc.vector.max(zs[:, p, :], z[:, p, :]).then_inc(zs_done, 1)
                dve.wait_ge(zs_done, t + 1)
                nc.vector.tensor_tensor_scan(cs[:, p, :], ones8[:, :], zs[:, p, :], -1.0, ALU.mult, ALU.add).then_inc(cs_done, 1)
                dve.wait_ge(cs_done, t + 1)
                nc.vector.tensor_tensor(tk[:, p, :], cs[:, p, :], inv_k, ALU.mult).then_inc(tk_done, 1)
                dve.wait_ge(tk_done, t + 1)
                nc.vector.tensor_reduce(tau[:, p:p + 1], tk[:, p, :], AX_X, ALU.max).then_inc(tau_done, 1)
                dve.wait_ge(tau_done, t + 1)
                nc.vector.tensor_scalar(wgt[:, p, :], z[:, p, :], tau[:, p:p + 1], 0.0,
                                        ALU.subtract, ALU.max).then_inc(wgt_done, 1)
                dve.wait_ge(hb_done, t + 1)
                dve.wait_ge(wgt_done, t + 1)
                nc.vector.tensor_tensor(g[:, p, :].rearrange("p (e r) -> p e r", e=E),
                                        hb[:, p, :].rearrange("p (e r) -> p e r", e=E),
                                        wgt[:, p, :].unsqueeze(2).broadcast_to([P, E, R]), ALU.mult).then_inc(g_done, 1)

            def lo_gT(t, p):
                dve.wait_ge(gT_hi_done, t + 1)
                nc.vector.tensor_tensor(gT_lo[:, p, :], ps_gT(p), gT_hi[:, p, :].bitcast(F32),
                                        ALU.subtract).then_inc(gT_lo_done, 1)

            def finish(t, p):
                dve.wait_ge(xab_done, t + 1)
                dve.wait_ge(out_mm, t + 1)
                nc.vector.tensor_tensor(xs[:, t, :].rearrange("p (h n) -> p h n", h=2), ps_out(p)[:, :, 0:BH],
                                        xs[:, t, :].rearrange("p (h n) -> p h n", h=2), ALU.add).then_inc(out_done, 1)

            def step(t, p, y_more=True):
                route(t, p)
                if y_more:
                    lo_y(t + 2, p, 0)
                lo_gT(t, p)
                if y_more:
                    lo_y(t + 2, p, 1)
                finish(t, p)

            with dve.Fori(0, LAST - 1, 2) as t:
                step(t, 0)
                step(t + 1, 1)
            step(LAST, 0, y_more=False)
            step(LAST + 1, 1, y_more=False)

        @block.tensor
        def _(pe):
            pe.wait_ge(cond_in, 16)
            nc.tensor.matmul(ps_h0, w0, embT, start=True, stop=True).then_inc(h0_mm, 1)
            pe.wait_ge(h0_done, 1)
            nc.tensor.matmul(ps_h1, w1, h0[:, :], start=True, stop=True).then_inc(h1_mm, 1)
            pe.wait_ge(h1_done, 1)
            nc.tensor.matmul(ps_lg, h1[:, :], w2, start=True, stop=True).then_inc(lg_mm, 1)
            pe.wait_ge(att_stacked, 2)
            pe.wait_ge(const_in, 16)
            nc.tensor.transpose(ps_attT, att_st[:, :, :].rearrange("b c k -> b (c k)"), ident).then_inc(att_mm, 1)
            pe.wait_ge(attT_done, 1)
            pe.wait_ge(wk_st_done, 1)
            for n in range(NG):
                mm = nc.tensor.matmul(ps_agg[:, n, :], wk_st[:, n * P:(n + 1) * P], attT[:, :], start=True, stop=True)
            mm.then_inc(agg_mm, 1)
            nc.tensor.matmul(ps_abias, wk_st[:, NG * P:], attT[:, :], start=True, stop=True).then_inc(abias_mm, 1)

            def mix(t, p, before=True):
                if before:
                    pe.wait_ge(y_lo_done, t)
                pe.wait_ge(mixm_done, t + 1)
                pe.wait_ge(x_lo_done, t + 1)
                mh = mixm[:, p, :, :, :].rearrange("p h s o -> p (h s o)")
                for c in range(C):
                    xh, xl = x_hi[:, p, c * P:(c + 1) * P], x_lo[:, p, c * P:(c + 1) * P]
                    nc.tensor.matmul(ps_y[:, c, :, :].rearrange("p m n -> p (m n)"), xh, mh, start=True, stop=True)
                    mm = nc.tensor.matmul(ps_y[:, c, 1, :], xl, mh[:, 0:P], start=False, stop=True, skip_group_check=True)
                mm.then_inc(y_mm, 1)

            def project(p, chunks):
                for c in chunks:
                    for n, (a, b) in enumerate(((y_hi, proj_hi), (y_hi, proj_lo), (y_lo, proj_hi))):
                        for h in range(2):
                            mm = nc.tensor.matmul(ps_out(p)[:, h, 0:HALF], a[:, p, c, :], b[:, c, h, :],
                                                  start=(c == 0 and n == 0), stop=(c == C - 1 and n == 2))
                return mm

            def transpose_g(t, p):
                pe.wait_ge(g_done, t + 1)
                nc.tensor.transpose(ps_gT(p), g[:, p, :], ident).then_inc(gT_mm, 1)

            def lora_out(t, p):
                pe.wait_ge(gT_lo_done, t + 1)
                for n, (a, b) in enumerate(((gT_hi, lb_hi), (gT_hi, lb_lo), (gT_lo, lb_hi))):
                    for h in range(2):
                        mm = nc.tensor.matmul(ps_out(p)[:, h, 0:BH], a[:, p, :], b[:, h * BH:(h + 1) * BH],
                                              start=False, stop=(n == 2), skip_group_check=True)
                mm.then_inc(out_mm, 1)

            def step(t, p, before=True, more=True):
                pe.wait_ge(y_lo_done, t + 1)
                if before == "far":
                    pe.wait_ge(out_done, t - 1)
                project(p, range(0, 2))
                if before:
                    transpose_g(t - 1, 1 - p)
                project(p, range(2, 3))
                if before:
                    lora_out(t - 1, 1 - p)
                project(p, range(3, C)).then_inc(proj_mm, 1)
                if more:
                    mix(t + 2, p)

            mix(0, 0, before=False)
            pe.wait_ge(ones_set, 2)
            for c in range(C):
                pe.wait_ge(proj_lo_done[c], 1)
                for part in (proj_hi, proj_lo):
                    for h in range(2):
                        mm = nc.tensor.matmul(ps_csum[:, h, :], ones_r[:, :], part[:, c, h, :],
                                              start=(c == 0 and part is proj_hi), stop=(c == C - 1 and part is proj_lo))
            mm.then_inc(csum_mm, 1)
            mix(1, 1)
            pe.wait_ge(csum_done, 1)
            pe.wait_ge(agg_f_act, 2)
            pe.wait_ge(agg_f_dve, 2)
            pe.wait_ge(lb_lo_done, 1)
            step(0, 0, before=False)
            step(1, 1)
            with pe.Fori(FIRST, LAST - 1, 2) as t:
                step(t, 0, before="far")
                step(t + 1, 1, before="far")
            step(LAST, 0, before="far", more=False)
            step(LAST + 1, 1, before="far", more=False)
            transpose_g(LAST + 1, 1)
            lora_out(LAST + 1, 1)


def kernel(x, cond_128, L0_cond_W0, L0_cond_b0, L0_cond_W1, L0_cond_b1, L0_cond_W2, L0_cond_b2, L0_cond_weight,
           L0_cond_bias_k, L0_ffn_W_base, L0_ffn_b_base, L0_ffn_W_router, L0_ffn_b_router, L0_ffn_lora_A,
           L0_ffn_lora_B):
    import numpy as np
    import concourse.bacc as bacc
    from concourse.bass_utils import run_bass_kernel_spmd

    x = np.asarray(x)
    S, ch, D = x.shape
    E, _, R = L0_ffn_lora_A.shape
    K = L0_cond_W2.shape[1]
    wbT = np.asarray(L0_ffn_W_base).T.reshape(D, 2, D // 2)
    la = np.asarray(L0_ffn_lora_A).transpose(1, 0, 2).reshape(D, 2, E * R // 2)
    wrT = np.asarray(L0_ffn_W_router).T.reshape(D, 2, E // 2)
    proj = np.concatenate([wbT, la, wrT], axis=2).reshape(D // 128, 128, -1).transpose(1, 0, 2).reshape(128, -1)
    def rows(v):
        return np.repeat(np.asarray(v)[None], 128, axis=0)

    cond = np.concatenate([np.asarray(cond_128).T, np.asarray(L0_cond_W0), np.asarray(L0_cond_W1),
                           np.asarray(L0_cond_W2), rows(L0_cond_b2), rows(L0_ffn_b_router),
                           np.asarray(L0_cond_b0)[:, None], np.asarray(L0_cond_b1)[:, None]], axis=1)
    wk = np.concatenate([np.asarray(L0_cond_weight).reshape(K, -1)] + [np.asarray(L0_cond_bias_k)] * (128 // ch), axis=1)
    wk = np.concatenate([wk] * 4, axis=0)
    b_row = np.asarray(L0_ffn_b_base)[None]
    lora_b = np.asarray(L0_ffn_lora_B).reshape(E * R, D)
    consts = np.zeros((128, 128 + E + 1), np.float32)
    consts[:, :128] = np.eye(128, dtype=np.float32)
    consts[:, 128:128 + E] = np.float32(1.0) / np.arange(1, E + 1, dtype=np.float32)
    for c in (1, 3):
        consts[c * K:(c + 1) * K, 128 + E] = -1.0

    arrays = {"x_in_dram": x.reshape(S * ch, D), "cond_dram": cond, "wk_dram": wk, "proj_dram": proj,
              "b_row_dram": b_row, "lora_b_dram": lora_b, "consts_dram": consts}
    arrays = {n: np.ascontiguousarray(a) for n, a in arrays.items()}
    nc = bacc.Bacc("TRN2", target_bir_lowering=False, num_devices=1)
    args = [nc.dram_tensor(n, a.shape, mybir.dt.from_np(a.dtype), kind="ExternalInput").ap() for n, a in arrays.items()]
    args.append(nc.dram_tensor("out_dram", (S * ch, D), F32, kind="ExternalOutput").ap())
    adaln_ffn_program(nc, *args)
    r = run_bass_kernel_spmd(nc, [arrays], core_ids=[0])
    return r.results[0]["out_dram"].reshape(S, ch, D)
```

```python
from contextlib import ExitStack

import concourse.bass as bass
from concourse import mybir

F32 = mybir.dt.float32
F32R = mybir.dt.float32r
ALU = mybir.AluOpType
ACT = mybir.ActivationFunctionType
AX_X = mybir.AxisListType.X

LEAST = -3.4028235e38
P = 128
CH = 32
SPT = P // CH


def adaln_ffn_program(nc: bass.Bass, x, cond, wk, proj, b_row, lora_b, consts, out):
    TOK, D = x.shape
    TILES = TOK // P
    C = D // P
    B = TOK // CH
    K = wk.shape[0] // 4
    HALF = proj.shape[1] // C // 2
    E = 8
    ER = lora_b.shape[0]
    R = ER // E
    BH, HH, EH = D // 2, ER // 2, E // 2
    assert HALF == BH + HH + EH and ER == P
    OG = P // CH
    NG = CH // OG
    POOL_CHUNKS, DVE_CHUNKS = (0, 2), (1, 3)
    EARLY = 6
    FIRST, LAST = 2, TILES - 2
    AHEAD = 8

    ctx = ExitStack()
    with ctx:
        def sb(name, shape, dt=F32):
            return ctx.enter_context(nc.sbuf_tensor(name, shape, dt))

        def sem(name):
            return ctx.enter_context(nc.semaphore(name))

        xs = sb("xs", [P, TILES, D])
        x_hi = sb("x_hi", [P, 2, D], F32R)
        x_lo = sb("x_lo", [P, 2, D], F32R)
        agg = sb("agg", [P, TILES, 2, CH], F32R)
        agg_f = sb("agg_f", [P, TILES, CH])
        mixm = sb("mixm", [P, 2, 2, SPT, CH], F32R)
        y_hi = sb("y_hi", [P, 2, C, P], F32R)
        y_lo = sb("y_lo", [P, 2, C, P], F32R)
        y_tmp = sb("y_tmp", [P, C, P])
        proj_raw = sb("proj_raw", [P, C, 2, HALF])
        proj_hi = sb("proj_hi", [P, C, 2, HALF], F32R)
        proj_lo = sb("proj_lo", [P, C, 2, HALF], F32R)
        lb_raw = sb("lb_raw", [P, D])
        lb_hi = sb("lb_hi", [P, D], F32R)
        lb_lo = sb("lb_lo", [P, D], F32R)
        csum = sb("csum", [P, 2, HALF])
        ones_r = sb("ones_r", [P, P], F32R)
        ones8 = sb("ones8", [P, E])
        b_base = sb("b_base", [P, D])
        ab_row = sb("ab_row", [P, 2, D])
        warm = sb("warm", [P, 1])
        cond_sb = sb("cond_sb", [P, cond.shape[1]])
        const_sb = sb("const_sb", [P, consts.shape[1]])
        wk_raw = sb("wk_raw", [4 * K, wk.shape[1]])
        wk_hi = sb("wk_hi", [4 * K, wk.shape[1]], F32R)
        wk_st = sb("wk_st", [4 * K, wk.shape[1]], F32R)
        h0 = sb("h0", [P, B])
        h1 = sb("h1", [P, B])
        lg = sb("lg", [B, K])
        nmx = sb("nmx", [B, 1])
        ex = sb("ex", [B, K])
        esum = sb("esum", [B, 1])
        rsum = sb("rsum", [B, 1])
        att_st = sb("att_st", [B, 4, K], F32R)
        attT = sb("attT", [4 * K, B], F32R)
        abias = sb("abias", [P, TILES, 1])
        zb = sb("zb", [P, TILES, E])
        z = sb("z", [P, 2, E])
        zs = sb("zs", [P, 2, E])
        cs = sb("cs", [P, 2, E])
        tau_k = sb("tau_k", [P, 2, E])
        tau = sb("tau", [P, 2])
        wgt = sb("wgt", [P, 2, E])
        hb = sb("hb", [P, 2, ER])
        g = sb("g", [P, 2, ER])
        gT_hi = sb("gT_hi", [P, 2, P], F32R)
        gT_lo = sb("gT_lo", [P, 2, P], F32R)

        at = 0

        def columns(n, tile):
            nonlocal at
            at += n
            return tile[:, at - n:at]

        embT, w0, w1, w2, b2, b_router, b0, b1 = (columns(n, cond_sb) for n in (B, P, P, K, K, E, 1, 1))
        at = 0
        ident, inv_k, neg_lo = (columns(n, const_sb) for n in (P, E, 1))

        psA = ctx.enter_context(nc.psum_tensor("psA", [P, 4, 512], F32))
        psB = ctx.enter_context(nc.psum_tensor("psB", [P, 4, 512], F32))

        ps_y, ps_y1 = (psA[:, b:b + 2, :].rearrange("p b (c m n) -> p (b c) m n", c=C // 2, m=2) for b in (0, 2))

        def ps_gT(p):
            return psA[:, 2 + p, 0:P]

        def ps_out(p):
            return psB[:, 2 * p:2 * p + 2, :]

        def ps_small(p):
            return ps_out(p)[:, :, BH:HALF]

        ps_small_last = psA[:, 0, 0:2 * (HALF - BH)].rearrange("p (h n) -> p h n", h=2)

        ps_h0, ps_h1, ps_lg = psA[:, 2, 0:B], psA[:, 3, 0:B], psA[:, 2, 128:128 + K]
        ps_attT, ps_abias = psA[0:4 * K, 3, 128:128 + B], psA[:, 2, 256:256 + B]
        ps_csum = psB[:, 0:2, 0:HALF]
        ps_agg = psB[:, 2:4, :].rearrange("p c (g b) -> p (c g) b", b=B)

        cond_in, wk_in, b_row_in, const_in, lb_in = (sem(n) for n in ("cond_in", "wk_in", "b_row_in", "const_in", "lb_in"))
        proj_in = [sem(f"proj_in{c}") for c in range(C)]
        warm_set, warmed = sem("warm_set"), sem("warmed")
        x_in = [sem("x_in_even"), sem("x_in_odd")]
        stored = sem("stored")
        ones_set = sem("ones_set")
        h0_mm, h0_done, h1_mm, h1_done, lg_mm = (sem(n) for n in ("h0_mm", "h0_done", "h1_mm", "h1_done", "lg_mm"))
        soft, exp_done, att_stacked = sem("soft"), sem("exp_done"), sem("att_stacked")
        att_mm, attT_done, abias_mm, abias_done = (sem(n) for n in ("att_mm", "attT_done", "abias_mm", "abias_done"))
        wk_hi_done, wk_st_done = sem("wk_hi_done"), sem("wk_st_done")
        mixm_half_done = sem("mixm_half_done")
        mixm_zeroed, agg_f_act, agg_f_dve = sem("mixm_zeroed"), sem("agg_f_act"), sem("agg_f_dve")
        proj_hi_done, csum_mm, csum_done = (sem(n) for n in ("proj_hi_done", "csum_mm", "csum_done"))
        proj_lo_done = [sem(f"proj_lo_done{c}") for c in range(C)]
        lb_hi_done, lb_lo_done = sem("lb_hi_done"), sem("lb_lo_done")
        zb_part, zb_done = sem("zb_part"), sem("zb_done")
        agg_mm, agg_hi_done, agg_lo_done = sem("agg_mm"), sem("agg_hi_done"), sem("agg_lo_done")
        x_hi_done, x_lo_done, x_ab_done, x_sum_done = (sem(n) for n in ("x_hi_done", "x_lo_done", "x_ab_done", "x_sum_done"))
        mixm_done, ab_row_done, y_tmp_done = sem("mixm_done"), sem("ab_row_done"), sem("y_tmp_done")
        y_mm, y_hi_done, y_lo_done = sem("y_mm"), sem("y_hi_done"), sem("y_lo_done")
        proj_mm, g_done, gT_mm, gT_hi_done, gT_lo_done = (sem(n) for n in ("proj_mm", "g_done", "gT_mm", "gT_hi_done", "gT_lo_done"))
        out_mm, out_done = sem("out_mm"), sem("out_done")
        z_done, zs_done, cs_done, tau_done, wgt_done = (sem(n) for n in ("z_done", "zs_done", "cs_done", "tau_done", "wgt_done"))
        y_half_mm, y_half_hi, y_half_tmp, y_half_lo = (sem(n) for n in ("y_half_mm", "y_half_hi", "y_half_tmp", "y_half_lo"))
        half_mm, half_done = sem("half_mm"), sem("half_done")

        x_t = x.rearrange("(t p) d -> t p d", p=P)
        out_t = out.rearrange("(t p) d -> t p d", p=P)

        def landed(t, p):
            return (t - p) * 8 + 16

        block = ctx.enter_context(nc.Block())

        @block.sync
        def _(sp):
            def load(t, p, first=False):
                if not first:
                    sp.wait_ge(x_in[p], landed(t, p) - 16)
                sp.dma_start(xs[:, t, :], x_t[t]).then_inc(x_in[p], 16)

            def store(t):
                sp.wait_ge(out_done, t + 1)
                sp.dma_start(out_t[t], xs[:, t, :]).then_inc(stored, 16)

            sp.dma_start(cond_sb[:, :], cond).then_inc(cond_in, 16)
            sp.dma_start(wk_raw[:, :], wk).then_inc(wk_in, 16)
            sp.dma_start(const_sb[:, :], consts).then_inc(const_in, 16)
            load(0, 0, first=True)
            for c in range(C):
                sp.dma_start(proj_raw[:, c, :, :], proj[:, c * 2 * HALF:(c + 1) * 2 * HALF]
                             .rearrange("p (h n) -> p h n", h=2)).then_inc(proj_in[c], 16)
            load(1, 1, first=True)
            sp.dma_start(lb_raw[:, :], lora_b).then_inc(lb_in, 16)
            sp.dma_start(b_base[:, :], b_row.broadcast_to([P, D])).then_inc(b_row_in, 16)
            with sp.Fori(2, AHEAD - 1, 2) as t:
                load(t, 0)
                load(t + 1, 1)
            with sp.Fori(0, TILES - AHEAD - 1, 2) as t:
                load(t + AHEAD, 0)
                load(t + AHEAD + 1, 1)
                store(t)
                store(t + 1)
            with sp.Fori(TILES - AHEAD, TILES - 1) as t:
                store(t)
            for h in range(2):
                sp.wait_ge(half_done, h + 1)
                half = slice(h * BH, (h + 1) * BH)
                sp.dma_start(out_t[TILES - 1][:, half], xs[:, TILES - 1, half]).then_inc(stored, 16)
            sp.wait_ge(stored, 16 * (TILES + 1))

        @block.gpsimd
        def _(pool):
            nc.gpsimd.memset(warm[:, :], 0.0).then_inc(warm_set, 1)
            nc.gpsimd.memset(ones_r[:, :].bitcast(F32), 1.0).then_inc(ones_set, 1)
            nc.gpsimd.memset(ones8[:, :], 1.0).then_inc(ones_set, 1)
            nc.gpsimd.memset(mixm[:, :, :, :, :].bitcast(F32), 0.0).then_inc(mixm_zeroed, 1)

            def lo_x(t, p):
                nc.gpsimd.tensor_tensor(x_lo[:, p, :], xs[:, t, :], x_hi[:, p, :].bitcast(F32),
                                        ALU.subtract).then_inc(x_lo_done, 1)

            def residual(t, p):
                nc.gpsimd.tensor_tensor(xs[:, t, :], xs[:, t, :], ab_row[:, p, :], ALU.add).then_inc(x_ab_done, 1)
                pool.wait_ge(b_row_in, 16)
                pool.wait_ge(x_ab_done, t + 1)
                nc.gpsimd.tensor_tensor(xs[:, t, :], xs[:, t, :], b_base[:, :], ALU.add).then_inc(x_sum_done, 1)

            def split_and_add(t, p):
                pool.wait_ge(x_hi_done, t + 3)
                pool.wait_ge(y_mm, t + 1)
                pool.wait_ge(ab_row_done, t + 1)
                lo_x(t + 2, p)
                residual(t, p)

            pool.wait_ge(x_hi_done, 1)
            lo_x(0, 0)
            for c in POOL_CHUNKS:
                pool.wait_ge(proj_hi_done, c + 1)
                nc.gpsimd.tensor_tensor(proj_lo[:, c, :, :], proj_raw[:, c, :, :],
                                        proj_hi[:, c, :, :].bitcast(F32), ALU.subtract).then_inc(proj_lo_done[c], 1)
            pool.wait_ge(x_hi_done, 2)
            lo_x(1, 1)
            pool.wait_ge(abias_done, SPT)
            pool.wait_ge(csum_done, 1)
            for h in range(2):
                zh = zb[:, :, EH * h:EH * h + EH]
                nc.gpsimd.tensor_tensor(zh, abias[:, :, :].broadcast_to([P, TILES, EH]),
                                        csum[:, h, BH + HH:HALF].unsqueeze(1).broadcast_to([P, TILES, EH]),
                                        ALU.mult).then_inc(zb_part, 1)
            pool.wait_ge(zb_part, 2)
            nc.gpsimd.tensor_tensor(zb[:, :, :], zb[:, :, :], b_router.unsqueeze(1).broadcast_to([P, TILES, E]),
                                    ALU.add).then_inc(zb_done, 1)
            pool.wait_ge(x_hi_done, 3)
            pool.wait_ge(y_mm, 1)
            lo_x(2, 0)
            pool.wait_ge(lb_hi_done, 1)
            nc.gpsimd.tensor_tensor(lb_lo[:, :], lb_raw[:, :], lb_hi[:, :].bitcast(F32), ALU.subtract).then_inc(lb_lo_done, 1)
            pool.wait_ge(ab_row_done, 1)
            residual(0, 0)
            pool.wait_ge(x_hi_done, 4)
            pool.wait_ge(y_mm, 2)
            lo_x(3, 1)
            pool.wait_ge(ab_row_done, 2)
            residual(1, 1)
            with pool.Fori(FIRST, LAST - 1, 2) as t:
                split_and_add(t, 0)
                split_and_add(t + 1, 1)
            for t in (LAST, LAST + 1):
                pool.wait_ge(ab_row_done, t + 1)
                residual(t, t % 2)

        @block.scalar
        def _(act):
            def hi_x(t, p, first=False):
                act.wait_ge(x_in[p], landed(t, p))
                if not first:
                    act.wait_ge(y_mm, t - 1)
                nc.scalar.copy(x_hi[:, p, :], xs[:, t, :]).then_inc(x_hi_done, 1)

            def hi_y(t, p, ps=ps_y):
                act.wait_ge(y_mm, t + 1)
                nc.scalar.copy(y_hi[:, p, :, :], ps[:, :, 0, :]).then_inc(y_hi_done, 1)

            def hi_y_first():
                act.wait_ge(y_half_mm, 1)
                nc.scalar.copy(y_hi[:, 0, 0:C // 2, :], ps_y[:, 0:C // 2, 0, :]).then_inc(y_half_hi, 1)
                act.wait_ge(y_mm, 1)
                nc.scalar.copy(y_hi[:, 0, C // 2:C, :], ps_y[:, C // 2:C, 0, :]).then_inc(y_hi_done, 1)

            def spread_mix(t, p, first=False, samples=range(SPT)):
                if not first:
                    act.wait_ge(y_mm, t - 1)
                for s in samples:
                    q = slice(CH * s, CH * s + CH)
                    cp = nc.scalar.copy(mixm[q, p, :, s, :], agg[q, t, :, :].bitcast(F32))
                cp.then_inc(mixm_done, 1)

            def scale_csum(t, p, first=False):
                if not first:
                    act.wait_ge(x_sum_done, t - 1)
                nc.scalar.activation(ab_row[:, p, :].rearrange("p (h n) -> p h n", h=2), csum[:, :, 0:BH],
                                     ACT.Copy, scale=abias[:, t, :]).then_inc(ab_row_done, 1)

            def hi_gT(t, p):
                act.wait_ge(gT_mm, t + 1)
                nc.scalar.copy(gT_hi[:, p, :], ps_gT(p)).then_inc(gT_hi_done, 1)

            act.wait_ge(warm_set, 1)
            nc.scalar.activation(warm[:, :], warm[:, :], ACT.Gelu).then_inc(warmed, 1)
            act.wait_ge(cond_in, 16)
            act.wait_ge(h0_mm, 1)
            nc.scalar.activation(h0[:, :], ps_h0, ACT.Gelu, bias=b0).then_inc(h0_done, 1)
            act.wait_ge(h1_mm, 1)
            nc.scalar.activation(h1[:, :], ps_h1, ACT.Gelu, bias=b1).then_inc(h1_done, 1)
            act.wait_ge(warmed, 1)
            nc.scalar.activation(warm[:, :], warm[:, :], ACT.Exp).then_inc(warmed, 1)
            act.wait_ge(soft, 2)
            nc.scalar.activation(ex[:, :], lg[:, :], ACT.Exp, bias=nmx[:, :],
                                 accum_out=esum[:, :]).then_inc(exp_done, 1)
            for c in range(C):
                act.wait_ge(proj_in[c], 16)
                nc.scalar.copy(proj_hi[:, c, :, :], proj_raw[:, c, :, :]).then_inc(proj_hi_done, 1)

            def lay_out_agg(tiles):
                for j in range(OG // 2):
                    for s in range(SPT):
                        cp = nc.scalar.copy(agg_f[CH * s:CH * s + CH, tiles, :].rearrange("p t (g j) -> p j t g", j=OG)[:, j],
                                            ps_agg[CH * j:CH * j + CH].rearrange("p g (t s) -> p s t g", s=SPT)[:, s, tiles])
                cp.then_inc(agg_f_act, 1)

            def hi_agg(tiles, n):
                act.wait_ge(agg_f_act, n)
                act.wait_ge(agg_f_dve, 2 * n - 1)
                nc.scalar.copy(agg[:, tiles, 0, :], agg_f[:, tiles, :]).then_inc(agg_hi_done, 1)

            act.wait_ge(agg_mm, 1)
            lay_out_agg(slice(0, EARLY))
            hi_agg(slice(0, EARLY), 1)
            hi_x(1, 1, first=True)
            act.wait_ge(mixm_zeroed, 1)
            act.wait_ge(agg_lo_done, 1)
            spread_mix(0, 0, first=True, samples=range(SPT // 2))
            spread_mix(1, 1, first=True)
            hi_y_first()
            hi_x(2, 0)
            hi_y(1, 1, ps_y1)
            spread_mix(2, 0)
            act.wait_ge(csum_done, 1)
            act.wait_ge(abias_done, SPT)
            scale_csum(0, 0, first=True)
            act.wait_ge(lb_in, 16)
            nc.scalar.copy(lb_hi[:, :], lb_raw[:, :]).then_inc(lb_hi_done, 1)
            lay_out_agg(slice(EARLY, TILES))
            hi_x(3, 1)
            spread_mix(3, 1)
            hi_agg(slice(EARLY, TILES), 2)

            def step(t, p, y_more=True, x_more=True):
                if y_more:
                    hi_y(t + 2, p)
                if x_more:
                    hi_x(t + 4, p)
                hi_gT(t, p)
                if y_more:
                    scale_csum(t + 2, p)
                if x_more:
                    spread_mix(t + 4, p)

            hi_y(2, 0)
            hi_gT(0, 0)
            scale_csum(1, 1, first=True)
            hi_x(4, 0)
            scale_csum(2, 0)
            spread_mix(4, 0)
            step(1, 1)
            act.wait_ge(agg_lo_done, 2)
            with act.Fori(FIRST, TILES - 5, 2) as t:
                step(t, 0)
                step(t + 1, 1)
            step(TILES - 4, 0, x_more=False)
            step(TILES - 3, 1, x_more=False)
            step(TILES - 2, 0, y_more=False, x_more=False)
            step(TILES - 1, 1, y_more=False, x_more=False)

        @block.vector
        def _(dve):
            dve.wait_ge(wk_in, 16)
            nc.vector.tensor_copy(wk_hi[:, :], wk_raw[:, :]).then_inc(wk_hi_done, 1)
            dve.wait_ge(wk_hi_done, 1)
            dve.wait_ge(const_in, 16)
            nc.vector.scalar_tensor_tensor(wk_st[:, :], wk_hi[:, :].bitcast(F32), neg_lo[0:4 * K], wk_raw[:, :],
                                           ALU.mult, ALU.add).then_inc(wk_st_done, 1)
            dve.wait_ge(x_in[0], 16)
            nc.vector.tensor_copy(x_hi[:, 0, :], xs[:, 0, :]).then_inc(x_hi_done, 1)
            dve.wait_ge(lg_mm, 1)
            nc.vector.tensor_tensor(lg[:, :], ps_lg, b2, ALU.add).then_inc(soft, 1)
            dve.wait_ge(soft, 1)
            nc.vector.tensor_reduce(nmx[:, :], lg[:, :], AX_X, ALU.max, negate=True).then_inc(soft, 1)
            dve.wait_ge(exp_done, 1)
            nc.vector.reciprocal(rsum[:, :], esum[:, :]).then_inc(soft, 1)
            dve.wait_ge(soft, 3)
            ex2, hi2, lo2 = ex[:, :].unsqueeze(1).broadcast_to([B, 2, K]), att_st[:, 0:2, :], att_st[:, 2:4, :]
            nc.vector.tensor_scalar(hi2, ex2, rsum[:, :], None, ALU.mult).then_inc(att_stacked, 1)
            dve.wait_ge(att_stacked, 1)
            nc.vector.scalar_tensor_tensor(lo2, ex2, rsum[:, :], hi2.bitcast(F32), ALU.mult, ALU.subtract).then_inc(att_stacked, 1)
            dve.wait_ge(att_mm, 1)
            nc.vector.tensor_copy(attT[:, :], ps_attT).then_inc(attT_done, 1)

            quadrants = [(j, s) for j in range(OG // 2, OG) for s in range(SPT)]

            def lay_out_agg(tiles, pairs):
                for j, s in pairs:
                    cp = nc.vector.tensor_copy(agg_f[CH * s:CH * s + CH, tiles, :].rearrange("p t (g j) -> p j t g", j=OG)[:, j],
                                               ps_agg[CH * j:CH * j + CH].rearrange("p g (t s) -> p s t g", s=SPT)[:, s, tiles])
                cp.then_inc(agg_f_dve, 1)

            def lo_agg(tiles, n):
                dve.wait_ge(agg_hi_done, n)
                nc.vector.tensor_tensor(agg[:, tiles, 1, :], agg_f[:, tiles, :], agg[:, tiles, 0, :].bitcast(F32),
                                        ALU.subtract).then_inc(agg_lo_done, 1)

            def lo_proj(c):
                dve.wait_ge(proj_hi_done, c + 1)
                nc.vector.tensor_tensor(proj_lo[:, c, :, :], proj_raw[:, c, :, :], proj_hi[:, c, :, :].bitcast(F32),
                                        ALU.subtract).then_inc(proj_lo_done[c], 1)

            lo_proj(DVE_CHUNKS[0])
            dve.wait_ge(agg_mm, 1)
            lay_out_agg(slice(0, EARLY), quadrants)
            lo_proj(DVE_CHUNKS[1])
            lo_agg(slice(0, EARLY), 1)
            dve.wait_ge(mixm_zeroed, 1)
            dve.wait_ge(agg_lo_done, 1)
            for s in range(SPT // 2, SPT):
                q = slice(CH * s, CH * s + CH)
                nc.vector.tensor_copy(mixm[q, 0, :, s, :], agg[q, 0, :, :].bitcast(F32)).then_inc(mixm_half_done, 1)
            dve.wait_ge(abias_mm, 1)
            for s in range(SPT):
                q = slice(CH * s, CH * s + CH)
                nc.vector.tensor_copy(abias[q, :, 0], ps_abias[q].rearrange("p (t s) -> p s t", s=SPT)[:, s]).then_inc(abias_done, 1)

            def lo_y(t, p, part, ps=ps_y):
                if part == 0:
                    dve.wait_ge(y_hi_done, t + 1)
                    nc.vector.tensor_tensor(y_tmp[:, :, :], ps[:, :, 0, :], y_hi[:, p, :, :].bitcast(F32),
                                            ALU.subtract).then_inc(y_tmp_done, 1)
                else:
                    dve.wait_ge(y_tmp_done, t)
                    nc.vector.tensor_tensor(y_lo[:, p, :, :], ps[:, :, 1, :], y_tmp[:, :, :], ALU.add).then_inc(y_lo_done, 1)

            dve.wait_ge(csum_mm, 1)
            nc.vector.tensor_copy(csum[:, :, :], ps_csum).then_inc(csum_done, 1)
            lay_out_agg(slice(EARLY, TILES), quadrants[:1])
            for h, (hi, done) in enumerate(((y_half_hi, y_half_lo), (y_hi_done, y_lo_done))):
                cc = slice(h * C // 2, (h + 1) * C // 2)
                dve.wait_ge(hi, 1)
                nc.vector.tensor_tensor(y_tmp[:, cc, :], ps_y[:, cc, 0, :], y_hi[:, 0, cc, :].bitcast(F32),
                                        ALU.subtract).then_inc(y_half_tmp, 1)
                dve.wait_ge(y_half_tmp, h + 1)
                nc.vector.tensor_tensor(y_lo[:, 0, cc, :], ps_y[:, cc, 1, :], y_tmp[:, cc, :], ALU.add).then_inc(done, 1)
            dve.wait_ge(y_lo_done, 1)
            lo_y(1, 1, 0, ps_y1)
            lo_y(1, 1, 1, ps_y1)
            lay_out_agg(slice(EARLY, TILES), quadrants[1:])
            dve.wait_ge(zb_done, 1)

            def lo_gT(t, p):
                dve.wait_ge(gT_hi_done, t + 1)
                nc.vector.tensor_tensor(gT_lo[:, p, :], ps_gT(p), gT_hi[:, p, :].bitcast(F32),
                                        ALU.subtract).then_inc(gT_lo_done, 1)

            def route(t, p, ps, in_gap=None):
                dve.wait_ge(proj_mm, t + 1)
                nc.vector.scalar_tensor_tensor(hb[:, p, :].rearrange("p (h n) -> p h n", h=2), csum[:, :, BH:BH + HH],
                                               abias[:, t, :], ps[:, :, 0:HH],
                                               ALU.mult, ALU.add)
                nc.vector.tensor_tensor(z[:, p, :].rearrange("p (h e) -> p h e", h=2), ps[:, :, HH:HH + EH],
                                        zb[:, t, :].rearrange("p (h e) -> p h e", h=2), ALU.add).then_inc(z_done, 1)
                dve.wait_ge(ones_set, 2)
                dve.wait_ge(z_done, t + 1)
                nc.vector.max(zs[:, p, :], z[:, p, :]).then_inc(zs_done, 1)
                dve.wait_ge(zs_done, t + 1)
                nc.vector.tensor_tensor_scan(cs[:, p, :], ones8[:, :], zs[:, p, :], -1.0, ALU.mult, ALU.add).then_inc(cs_done, 1)
                if in_gap:
                    in_gap()
                dve.wait_ge(const_in, 16)
                dve.wait_ge(cs_done, t + 1)
                nc.vector.tensor_tensor_reduce(tau_k[:, p, :], cs[:, p, :], inv_k, 1.0, LEAST, ALU.mult, ALU.max,
                                               tau[:, p:p + 1]).then_inc(tau_done, 1)
                dve.wait_ge(tau_done, t + 1)
                nc.vector.tensor_scalar(wgt[:, p, :], z[:, p, :], tau[:, p:p + 1], 0.0,
                                        ALU.subtract, ALU.max).then_inc(wgt_done, 1)
                dve.wait_ge(wgt_done, t + 1)
                nc.vector.tensor_tensor(g[:, p, :].rearrange("p (e r) -> p e r", e=E),
                                        hb[:, p, :].rearrange("p (e r) -> p e r", e=E),
                                        wgt[:, p, :].unsqueeze(2).broadcast_to([P, E, R]), ALU.mult).then_inc(g_done, 1)

            def finish(t, p):
                dve.wait_ge(x_sum_done, t + 1)
                dve.wait_ge(out_mm, t + 1)
                nc.vector.tensor_tensor(xs[:, t, :].rearrange("p (h n) -> p h n", h=2), ps_out(p)[:, :, 0:BH],
                                        xs[:, t, :].rearrange("p (h n) -> p h n", h=2), ALU.add).then_inc(out_done, 1)

            def step(t, p):
                route(t, p, ps_small(p))
                lo_y(t + 2, p, 0)
                lo_gT(t, p)
                lo_y(t + 2, p, 1)
                finish(t, p)

            route(0, 0, ps_small(0))
            lo_agg(slice(EARLY, TILES), 2)
            lo_gT(0, 0)
            lo_y(2, 0, 0)
            lo_y(2, 0, 1)
            finish(0, 0)
            step(1, 1)
            with dve.Fori(FIRST, LAST - 1, 2) as t:
                step(t, 0)
                step(t + 1, 1)
            route(LAST, 0, ps_small(0))
            route(LAST + 1, 1, ps_small_last, in_gap=lambda: lo_gT(LAST, 0))
            lo_gT(LAST + 1, 1)
            finish(LAST, 0)
            dve.wait_ge(x_sum_done, TILES)
            for h in range(2):
                dve.wait_ge(half_mm, h + 1)
                xh = xs[:, TILES - 1, h * BH:(h + 1) * BH]
                nc.vector.tensor_tensor(xh, ps_out(1)[:, h, 0:BH], xh, ALU.add).then_inc(half_done, 1)

        @block.tensor
        def _(pe):
            def keep_busy(n):
                for _ in range(n):
                    nc.tensor.matmul(psA[:, 0, 0:2 * P], ones_r[:, :], mixm[:, 0, :, :, :].rearrange("p h s o -> p (h s o)"),
                                     start=True, stop=True)

            pe.wait_ge(ones_set, 2)
            pe.wait_ge(mixm_zeroed, 1)
            keep_busy(8)
            pe.wait_ge(cond_in, 16)
            nc.tensor.matmul(ps_h0, w0, embT, start=True, stop=True).then_inc(h0_mm, 1)
            keep_busy(4)
            pe.wait_ge(h0_done, 1)
            nc.tensor.matmul(ps_h1, w1, h0[:, :], start=True, stop=True).then_inc(h1_mm, 1)
            keep_busy(3)
            pe.wait_ge(h1_done, 1)
            nc.tensor.matmul(ps_lg, h1[:, :], w2, start=True, stop=True).then_inc(lg_mm, 1)
            keep_busy(7)
            pe.wait_ge(att_stacked, 2)
            pe.wait_ge(const_in, 16)
            nc.tensor.transpose(ps_attT, att_st[:, :, :].rearrange("b c k -> b (c k)").bitcast(F32), ident).then_inc(att_mm, 1)
            keep_busy(2)
            pe.wait_ge(attT_done, 1)
            pe.wait_ge(wk_st_done, 1)
            for n in range(NG):
                mm = nc.tensor.matmul(ps_agg[:, n, :], wk_st[:, n * P:(n + 1) * P], attT[:, :], start=True, stop=True)
            mm.then_inc(agg_mm, 1)
            nc.tensor.matmul(ps_abias, wk_st[:, NG * P:], attT[:, :], start=True, stop=True).then_inc(abias_mm, 1)

            def mix(t, p, ps=ps_y, first=False, halves=False):
                if not first:
                    pe.wait_ge(y_lo_done, t)
                pe.wait_ge(mixm_done, t + 1)
                pe.wait_ge(x_lo_done, t + 1)
                mh = mixm[:, p, :, :, :].rearrange("p h s o -> p (h s o)")
                for c in range(C):
                    xh, xl = x_hi[:, p, c * P:(c + 1) * P], x_lo[:, p, c * P:(c + 1) * P]
                    nc.tensor.matmul(ps[:, c, :, :].rearrange("p m n -> p (m n)"), xh, mh, start=True, stop=True)
                    mm = nc.tensor.matmul(ps[:, c, 1, :], xl, mh[:, 0:P], start=False, stop=True, skip_group_check=True)
                    if halves and c == C // 2 - 1:
                        mm.then_inc(y_half_mm, 1)
                mm.then_inc(y_mm, 1)

            def project(p, first, last, columns=HALF):
                for m in range(first, last):
                    c, n, h = m // 6, m % 6 // 2, m % 2
                    a, b = ((y_hi, proj_hi), (y_hi, proj_lo), (y_lo, proj_hi))[n]
                    mm = nc.tensor.matmul(ps_out(p)[:, h, 0:columns], a[:, p, c, :], b[:, c, h, 0:columns],
                                          start=(m < 2), stop=(m >= 6 * C - 2))
                return mm

            def transpose_g(t, p):
                pe.wait_ge(g_done, t + 1)
                nc.tensor.transpose(ps_gT(p), g[:, p, :], ident).then_inc(gT_mm, 1)

            def lora_out(t, p):
                pe.wait_ge(gT_lo_done, t + 1)
                for n, (a, b) in enumerate(((gT_hi, lb_hi), (gT_hi, lb_lo), (gT_lo, lb_hi))):
                    for h in range(2):
                        mm = nc.tensor.matmul(ps_out(p)[:, h, 0:BH], a[:, p, :], b[:, h * BH:(h + 1) * BH],
                                              start=False, stop=(n == 2), skip_group_check=True)
                mm.then_inc(out_mm, 1)

            def step(t, p, reused=True, more=True, transpose_at=10, lora_at=18):
                pe.wait_ge(y_lo_done, t + 1)
                if reused:
                    pe.wait_ge(out_done, t - 1)
                project(p, 0, transpose_at)
                transpose_g(t - 1, 1 - p)
                project(p, transpose_at, lora_at)
                lora_out(t - 1, 1 - p)
                project(p, lora_at, 6 * C).then_inc(proj_mm, 1)
                if more:
                    mix(t + 2, p)

            def column_sums(part, first, last):
                for c in range(C):
                    if part is proj_lo:
                        pe.wait_ge(proj_lo_done[c], 1)
                    else:
                        pe.wait_ge(proj_hi_done, c + 1)
                    for h in range(2):
                        mm = nc.tensor.matmul(ps_csum[:, h, :], ones_r[:, :], part[:, c, h, :],
                                              start=(first and c == 0), stop=(last and c == C - 1))
                return mm

            column_sums(proj_hi, True, False)
            column_sums(proj_lo, False, True).then_inc(csum_mm, 1)
            pe.wait_ge(mixm_half_done, SPT // 2)
            mix(0, 0, first=True, halves=True)
            pe.wait_ge(abias_done, SPT)
            mix(1, 1, ps_y1, first=True)
            pe.wait_ge(csum_done, 1)
            pe.wait_ge(y_half_lo, 1)
            project(0, 0, 3 * C)
            pe.wait_ge(y_lo_done, 1)
            project(0, 3 * C, 6 * C).then_inc(proj_mm, 1)
            mix(2, 0)
            pe.wait_ge(agg_f_act, 2)
            pe.wait_ge(agg_f_dve, 3)
            pe.wait_ge(lb_lo_done, 1)
            step(1, 1, reused=False, transpose_at=12, lora_at=20)
            with pe.Fori(FIRST, LAST - 1, 2) as t:
                step(t, 0)
                step(t + 1, 1)
            step(LAST, 0, more=False)
            pe.wait_ge(y_lo_done, TILES)
            for m in range(3 * C):
                c, (a, b) = m // 3, ((y_hi, proj_hi), (y_hi, proj_lo), (y_lo, proj_hi))[m % 3]
                mm = nc.tensor.matmul(ps_small_last, a[:, 1, c, :], b[:, c, :, BH:HALF], start=(m == 0), stop=(m == 3 * C - 1))
            mm.then_inc(proj_mm, 1)
            pe.wait_ge(out_done, TILES - 2)
            project(1, 0, 8, columns=BH)
            transpose_g(LAST, 0)
            project(1, 8, 14, columns=BH)
            lora_out(LAST, 0)
            transpose_g(LAST + 1, 1)
            project(1, 14, 6 * C, columns=BH)
            pe.wait_ge(gT_lo_done, TILES)
            for h in range(2):
                for n, (a, b) in enumerate(((gT_hi, lb_hi), (gT_hi, lb_lo), (gT_lo, lb_hi))):
                    mm = nc.tensor.matmul(ps_out(1)[:, h, 0:BH], a[:, 1, :], b[:, h * BH:(h + 1) * BH],
                                          start=False, stop=(n == 2), skip_group_check=True)
                mm.then_inc(half_mm, 1)


def kernel(x, cond_128, L0_cond_W0, L0_cond_b0, L0_cond_W1, L0_cond_b1, L0_cond_W2, L0_cond_b2, L0_cond_weight,
           L0_cond_bias_k, L0_ffn_W_base, L0_ffn_b_base, L0_ffn_W_router, L0_ffn_b_router, L0_ffn_lora_A,
           L0_ffn_lora_B):
    import numpy as np
    import concourse.bacc as bacc
    from concourse.bass_utils import run_bass_kernel_spmd

    x = np.asarray(x)
    S, ch, D = x.shape
    E, _, R = L0_ffn_lora_A.shape
    K = L0_cond_W2.shape[1]
    wbT = np.asarray(L0_ffn_W_base).T.reshape(D, 2, D // 2)
    la = np.asarray(L0_ffn_lora_A).transpose(1, 0, 2).reshape(D, 2, E * R // 2)
    wrT = np.asarray(L0_ffn_W_router).T.reshape(D, 2, E // 2)
    proj = np.concatenate([wbT, la, wrT], axis=2).reshape(D // 128, 128, -1).transpose(1, 0, 2).reshape(128, -1)
    def rows(v):
        return np.repeat(np.asarray(v)[None], 128, axis=0)

    cond = np.concatenate([np.asarray(cond_128).T, np.asarray(L0_cond_W0), np.asarray(L0_cond_W1),
                           np.asarray(L0_cond_W2), rows(L0_cond_b2), rows(L0_ffn_b_router),
                           np.asarray(L0_cond_b0)[:, None], np.asarray(L0_cond_b1)[:, None]], axis=1)
    wk = np.concatenate([np.asarray(L0_cond_weight).reshape(K, -1)] + [np.asarray(L0_cond_bias_k)] * (128 // ch), axis=1)
    wk = np.concatenate([wk] * 4, axis=0)
    b_row = np.asarray(L0_ffn_b_base)[None]
    lora_b = np.asarray(L0_ffn_lora_B).reshape(E * R, D)
    consts = np.zeros((128, 128 + E + 1), np.float32)
    consts[:, :128] = np.eye(128, dtype=np.float32)
    consts[:, 128:128 + E] = np.float32(1.0) / np.arange(1, E + 1, dtype=np.float32)
    for c in (1, 3):
        consts[c * K:(c + 1) * K, 128 + E] = -1.0

    arrays = {"x_in_dram": x.reshape(S * ch, D), "cond_dram": cond, "wk_dram": wk, "proj_dram": proj,
              "b_row_dram": b_row, "lora_b_dram": lora_b, "consts_dram": consts}
    arrays = {n: np.ascontiguousarray(a) for n, a in arrays.items()}
    nc = bacc.Bacc("TRN2", target_bir_lowering=False, num_devices=1)
    args = [nc.dram_tensor(n, a.shape, mybir.dt.from_np(a.dtype), kind="ExternalInput").ap() for n, a in arrays.items()]
    args.append(nc.dram_tensor("out_dram", (S * ch, D), F32, kind="ExternalOutput").ap())
    adaln_ffn_program(nc, *args)
    r = run_bass_kernel_spmd(nc, [arrays], core_ids=[0])
    return r.results[0]["out_dram"].reshape(S, ch, D)
```
